# Optimizing a Trainium2 kernel written in Bass

```python
import numpy as np
import jax
import jax.numpy as jnp

def _softmax(x, axis=-1):
    return jax.nn.softmax(x, axis=axis)

def _gelu(x):
    return jax.nn.gelu(x, approximate=True)

def _silu(x):
    return jax.nn.silu(x)

def _sigmoid(x):
    return jax.nn.sigmoid(x)

def _layernorm(x, axis=-1, eps=1e-05):
    m = jnp.mean(x, axis=axis, keepdims=True)
    v = jnp.var(x, axis=axis, keepdims=True)
    return (x - m) / jnp.sqrt(v + eps)

def _scatter_add(tgt, idx, src, axis=0):
    return tgt.at[idx].add(src)

def _segment_sum(src, seg, n):
    return jax.ops.segment_sum(src, seg, n)
kernel_name = 'mk_hybrid_d1_jaxref_r8_ac2b22'

def setup_inputs(seed: int=0):
    np.random.seed(seed)
    _w = jnp.asarray

    def _L0_attn_a_setup():
        import jax, jax.numpy as jnp
        import numpy as np
        DIM = 128
        DIM_HEADS = 128
        HEADS = 8
        DHEAD = DIM_HEADS // HEADS
        EPS = 1e-06

        def _l2norm(t, axis=-1):
            n = jnp.sqrt(jnp.sum(t * t, axis=axis, keepdims=True))
            return t / jnp.maximum(n, 1e-12)
        key = jax.random.key(seed)
        k1, k2, k3 = jax.random.split(key, 3)
        x = jax.random.normal(k1, (8, 512, DIM), dtype=jnp.float32)
        norm_weight = jnp.ones((DIM,), dtype=jnp.float32)
        w_qkv = jax.random.normal(k2, (3 * DIM_HEADS, DIM), dtype=jnp.float32) * (1.0 / np.sqrt(DIM))
        temperature = jnp.zeros((HEADS, 1, 1), dtype=jnp.float32)
        w_out = jax.random.normal(k3, (DIM, DIM_HEADS), dtype=jnp.float32) * (1.0 / np.sqrt(DIM_HEADS))
        return {'x': x, 'norm_weight': norm_weight, 'w_qkv': w_qkv, 'temperature': temperature, 'w_out': w_out}
    _L0_attn_a_in = _L0_attn_a_setup()

    def _L0_attn_b_setup():
        import jax, jax.numpy as jnp
        import numpy as np
        SPS_AMPLIFY = 1.5
        SPS_DAMPEN = 0.3
        SPS_DEEP_QUESTION = 0.1
        SPS_EXCLAIM = 0.85
        SPS_QUESTION = 0.25
        SPS_SUPER_EXCLAIM = 0.95
        B, S, D = (4, 256, 128)
        NUM_HEADS = 16
        HEAD_DIM = D // NUM_HEADS
        SCALE = HEAD_DIM ** (-0.5)

        def sps_pro(x):
            xn = jax.nn.sigmoid(x)
            mult = jnp.where(xn > SPS_SUPER_EXCLAIM, 2.0, jnp.where(xn > SPS_EXCLAIM, SPS_AMPLIFY, jnp.where(xn < SPS_DEEP_QUESTION, 0.1, jnp.where(xn < SPS_QUESTION, SPS_DAMPEN, 1.0))))
            return x * mult
        key = jax.random.key(seed)
        k0, k1, k2, k3, k4 = jax.random.split(key, 5)
        s = 1.0 / np.sqrt(D)
        return {'x': jax.random.normal(k0, (B, S, D), dtype=jnp.float32), 'W_qkv': jax.random.uniform(k1, (D, 3 * D), dtype=jnp.float32, minval=-s, maxval=s), 'b_qkv': jax.random.uniform(k2, (3 * D,), dtype=jnp.float32, minval=-s, maxval=s), 'W_proj': jax.random.uniform(k3, (D, D), dtype=jnp.float32, minval=-s, maxval=s), 'b_proj': jax.random.uniform(k4, (D,), dtype=jnp.float32, minval=-s, maxval=s)}
    _L0_attn_b_in = _L0_attn_b_setup()

    def _L0_ffn_setup():
        import jax, jax.numpy as jnp
        import numpy as np
        B, S, H, E, I, MAX_K, A_HID = (2, 256, 128, 8, 336, 6, 50)
        key = jax.random.key(seed)
        ks = jax.random.split(key, 10)
        sc = 0.02
        return {'hidden_states': jax.random.normal(ks[0], (B, S, H), dtype=jnp.float32), 'router_w': jax.random.normal(ks[1], (E, H), dtype=jnp.float32) * sc, 'actor_w1': jax.random.normal(ks[2], (A_HID, H), dtype=jnp.float32) * sc, 'actor_b1': jnp.zeros((A_HID,), dtype=jnp.float32), 'actor_w2': jax.random.normal(ks[3], (MAX_K, A_HID), dtype=jnp.float32) * sc, 'actor_b2': jnp.zeros((MAX_K,), dtype=jnp.float32), 'gate_w': jax.random.normal(ks[4], (E, I, H), dtype=jnp.float32) * sc, 'up_w': jax.random.normal(ks[5], (E, I, H), dtype=jnp.float32) * sc, 'down_w': jax.random.normal(ks[6], (E, H, I), dtype=jnp.float32) * sc}
    _L0_ffn_in = _L0_ffn_setup()
    _d = {'L0_attn_a_x': _L0_attn_a_in['x'], 'L0_attn_a_norm_weight': _L0_attn_a_in['norm_weight'], 'L0_attn_a_w_qkv': _L0_attn_a_in['w_qkv'], 'L0_attn_a_temperature': _L0_attn_a_in['temperature'], 'L0_attn_a_w_out': _L0_attn_a_in['w_out'], 'L0_attn_b_W_qkv': _L0_attn_b_in['W_qkv'], 'L0_attn_b_b_qkv': _L0_attn_b_in['b_qkv'], 'L0_attn_b_W_proj': _L0_attn_b_in['W_proj'], 'L0_attn_b_b_proj': _L0_attn_b_in['b_proj'], 'L0_ffn_router_w': _L0_ffn_in['router_w'], 'L0_ffn_actor_w1': _L0_ffn_in['actor_w1'], 'L0_ffn_actor_b1': _L0_ffn_in['actor_b1'], 'L0_ffn_actor_w2': _L0_ffn_in['actor_w2'], 'L0_ffn_actor_b2': _L0_ffn_in['actor_b2'], 'L0_ffn_gate_w': _L0_ffn_in['gate_w'], 'L0_ffn_up_w': _L0_ffn_in['up_w'], 'L0_ffn_down_w': _L0_ffn_in['down_w']}
    _x0 = _d['L0_attn_a_x']
    _d['L0_attn_a_x'] = jax.random.normal(jax.random.fold_in(jax.random.key(seed), 1), (4, 512, 128), dtype=_x0.dtype)
    del _x0
    return _d

def reference(L0_attn_a_x, L0_attn_a_norm_weight, L0_attn_a_w_qkv, L0_attn_a_temperature, L0_attn_a_w_out, L0_attn_b_W_qkv, L0_attn_b_b_qkv, L0_attn_b_W_proj, L0_attn_b_b_proj, L0_ffn_router_w, L0_ffn_actor_w1, L0_ffn_actor_b1, L0_ffn_actor_w2, L0_ffn_actor_b2, L0_ffn_gate_w, L0_ffn_up_w, L0_ffn_down_w):

    def _L0_attn_a_ref(x, norm_weight, w_qkv, temperature, w_out):
        import jax, jax.numpy as jnp
        import numpy as np
        DIM = 128
        DIM_HEADS = 128
        HEADS = 8
        DHEAD = DIM_HEADS // HEADS
        EPS = 1e-06

        def _l2norm(t, axis=-1):
            n = jnp.sqrt(jnp.sum(t * t, axis=axis, keepdims=True))
            return t / jnp.maximum(n, 1e-12)
        b, n, _ = x.shape
        ms = jnp.mean(x * x, axis=-1, keepdims=True)
        xn = x * jax.lax.rsqrt(ms + EPS) * norm_weight
        qkv = jnp.einsum('bnc,oc->bno', xn, w_qkv)
        qkv = qkv.reshape(b, n, 3, HEADS, DHEAD).transpose(2, 0, 3, 4, 1)
        q, k, v = (qkv[0], qkv[1], qkv[2])
        q = _l2norm(q)
        k = _l2norm(k)
        q = q * jnp.exp(temperature)
        sim = jnp.einsum('bhin,bhjn->bhij', q, k)
        attn = jax.nn.softmax(sim, axis=-1)
        out = jnp.einsum('bhij,bhjn->bhin', attn, v)
        out = out.transpose(0, 3, 1, 2).reshape(b, n, HEADS * DHEAD)
        return jnp.einsum('bnc,oc->bno', out, w_out)

    def _L0_attn_b_ref(x, W_qkv, b_qkv, W_proj, b_proj):
        import jax, jax.numpy as jnp
        import numpy as np
        SPS_AMPLIFY = 1.5
        SPS_DAMPEN = 0.3
        SPS_DEEP_QUESTION = 0.1
        SPS_EXCLAIM = 0.85
        SPS_QUESTION = 0.25
        SPS_SUPER_EXCLAIM = 0.95
        B, S, D = (4, 256, 128)
        NUM_HEADS = 16
        HEAD_DIM = D // NUM_HEADS
        SCALE = HEAD_DIM ** (-0.5)

        def sps_pro(x):
            xn = jax.nn.sigmoid(x)
            mult = jnp.where(xn > SPS_SUPER_EXCLAIM, 2.0, jnp.where(xn > SPS_EXCLAIM, SPS_AMPLIFY, jnp.where(xn < SPS_DEEP_QUESTION, 0.1, jnp.where(xn < SPS_QUESTION, SPS_DAMPEN, 1.0))))
            return x * mult
        qkv = jnp.einsum('bsd,de->bse', x, W_qkv) + b_qkv
        q, k, v = jnp.split(qkv, 3, axis=-1)
        attn = jnp.einsum('bsd,btd->bst', q, k) * SCALE
        attn = sps_pro(attn)
        attn = jax.nn.softmax(attn, axis=-1)
        out = jnp.einsum('bst,btd->bsd', attn, v)
        out = jnp.einsum('bsd,de->bse', out, W_proj) + b_proj
        return out

    def _L0_ffn_ref(hidden_states, router_w, actor_w1, actor_b1, actor_w2, actor_b2, gate_w, up_w, down_w):
        import jax, jax.numpy as jnp
        import numpy as np
        B, S, H, E, I, MAX_K, A_HID = (2, 256, 128, 8, 336, 6, 50)
        probs = jax.nn.softmax(jnp.einsum('bsh,eh->bse', hidden_states, router_w).astype(jnp.float32), axis=-1)
        a_h = jax.nn.gelu(jnp.einsum('bsh,ah->bsa', hidden_states, actor_w1) + actor_b1)
        actor_logits = jnp.clip(jnp.einsum('bsa,ka->bsk', a_h, actor_w2) + actor_b2, -30.0, 30.0)
        sampled_k = jnp.argmax(actor_logits, axis=-1) + 1
        order = jnp.argsort(-probs, axis=-1)
        rank = jnp.argsort(order, axis=-1)
        mask = rank < sampled_k[..., None]
        scores = jnp.where(mask, probs, 0.0).astype(hidden_states.dtype)
        out = jnp.zeros_like(hidden_states)
        for e in range(E):
            g = jnp.einsum('bsh,ih->bsi', hidden_states, gate_w[e])
            u = jnp.einsum('bsh,ih->bsi', hidden_states, up_w[e])
            y = jnp.einsum('bsi,hi->bsh', jax.nn.silu(g) * u, down_w[e])
            out = out + scores[..., e:e + 1] * y
        return out
    x = L0_attn_a_x
    x = x + _L0_attn_a_ref(_layernorm(x, axis=-1), L0_attn_a_norm_weight, L0_attn_a_w_qkv, L0_attn_a_temperature, L0_attn_a_w_out)
    x = x + _L0_ffn_ref(_layernorm(x, axis=-1), L0_ffn_router_w, L0_ffn_actor_w1, L0_ffn_actor_b1, L0_ffn_actor_w2, L0_ffn_actor_b2, L0_ffn_gate_w, L0_ffn_up_w, L0_ffn_down_w)
    x = x + _L0_attn_b_ref(_layernorm(x, axis=-1), L0_attn_b_W_qkv, L0_attn_b_b_qkv, L0_attn_b_W_proj, L0_attn_b_b_proj)
    x = x + _L0_ffn_ref(_layernorm(x, axis=-1), L0_ffn_router_w, L0_ffn_actor_w1, L0_ffn_actor_b1, L0_ffn_actor_w2, L0_ffn_actor_b2, L0_ffn_gate_w, L0_ffn_up_w, L0_ffn_down_w)
    return x

_drawn_inputs = setup_inputs


def setup_inputs(seed=0):
    import zlib

    import numpy as np

    out = dict(_drawn_inputs(seed))
    spreads = {'L0_attn_a_norm_weight': (1.0, 0.2),
     'L0_attn_a_temperature': (0.0, 0.8),
     'L0_ffn_actor_b1': (0.0, 0.8),
     'L0_ffn_actor_b2': (0.0, 0.8)}
    factors = {'L0_ffn_router_w': 8.0,
     'L0_ffn_actor_w1': 8.0,
     'L0_ffn_actor_w2': 8.0,
     'L0_ffn_gate_w': 8.0,
     'L0_ffn_up_w': 8.0,
     'L0_ffn_down_w': 8.0}
    for name, (base, spread) in spreads.items():
        noise = np.random.default_rng([zlib.crc32(name.encode()), seed]).standard_normal(out[name].shape)
        drawn = base * np.exp(spread * noise) if base else spread * noise
        out[name] = jnp.asarray(drawn.astype(out[name].dtype))
    for name, factor in factors.items():
        out[name] = (out[name] * factor).astype(out[name].dtype)
    return out
```

```python
from contextlib import ExitStack

import concourse.bass as bass
from concourse import mybir

F32 = mybir.dt.float32
F32R = mybir.dt.float32r
BF16 = mybir.dt.bfloat16
I32 = mybir.dt.int32
ALU = mybir.AluOpType
ACT = mybir.ActivationFunctionType
AX_X = mybir.AxisListType.X

P = 128
NB = 4
T = 512
NT = T // P
D = 128
H, DH = 8, 16
E, I, CH = 8, 336, 21
KMAX, AH = 6, 50
LN_EPS, RMS_EPS = 1e-5, 1e-6
B_SCALE = 8 ** -0.5
X10, X25, X85, X95 = (-2.1972245773362196, -1.0986122886681098, 1.7346010553881064, 2.9444389791664403)
RSQRT_SEED = 1597463007.0
LAG = 3
WCH = 3
WCOLS = WCH * P
NSTAGE = 6
NEG = -1e30

C_QKV, C_OUT, C_BQKV, C_BPROJ, C_ROUTER, C_ACTOR = 0, 384, 512, 896, 1024, 1032
C_ALL = C_ACTOR + P


def plan():
    seq = [0]

    def norm(kind, b, which):
        n = seq[0]
        seq[0] += which == "xT"
        return which, n, kind, b

    def attention_a(b):
        return [[norm("A", b, "stats")], [norm("A", b, "xn"), norm("A", b, "xT")], [("aqkv", b)], [("asim", b)],
                [("aexp", b)], [("aT", b)], [("aav", b)], [("y", b)]]

    steps = []
    add = lambda *s: steps.extend(s)
    for part in attention_a(0):
        add(*part)
    add(*[("wp", j) for j in range(6)])
    add(norm("F", 0, "stats"), norm("F", 0, "xn"), norm("F", 0, "xT"), ("route", 0), ("gelu", 0), ("act", 0), ("sbc", 0))
    piece = 6
    for n in range(2 * NB):
        a = n + 1
        b = n - 1
        for c in range(CH):
            k = CH * n + c
            add(("gu", k))
            if k >= LAG:
                add(("down", k - LAG))
            if k:
                add(("hl", k - 1))
            if piece < 3 * CH // WCH:
                add(("wp", piece))
                piece += 1
            if a < NB:
                if c == 0:
                    add(norm("A", a, "stats"))
                if c == 1:
                    add(norm("A", a, "xn"), norm("A", a, "xT"))
                if c == 2:
                    add(("aqkv", a))
                if c == 3:
                    add(("asim", a))
                if c == 4:
                    add(("aexp", a))
                if c == 5:
                    add(("aT", a))
                if c == 6:
                    add(("aav", a))
                if c == 7:
                    add(("y", a))
            if c == 3 and n:
                add(("yT", n - 1))
            if 0 <= b < NB:
                if c == 4:
                    add(norm("B", b, "stats"))
                if c == 5:
                    add(norm("B", b, "xn"), norm("B", b, "xT"))
                if c == 6:
                    add(("bqkv", b))
                if c in (7, 8):
                    add(("bs", b, 2 * (c - 7)), ("bs", b, 2 * (c - 7) + 1))
                if c in (9, 11, 13, 15):
                    add(("bsp", b, (c - 9) // 2))
                if c == 16:
                    add(("bexp", b))
                if c in (17, 18):
                    add(("bpT", b, 2 * (c - 17)), ("bpT", b, 2 * (c - 17) + 1))
                if c == 19:
                    add(("bo", b))
                if c == 20:
                    add(("by", b))
            if n + 1 < 2 * NB:
                if c == 8:
                    add(norm("F", n + 1, "stats"))
                if c == 10:
                    add(norm("F", n + 1, "xn"), norm("F", n + 1, "xT"))
                if c == 12:
                    add(("route", n + 1))
                if c == 16:
                    add(("gelu", n + 1))
                if c == 18:
                    add(("act", n + 1))
                if c == 20:
                    add(("sbc", n + 1))
    last = CH * 2 * NB
    add(("hl", last - 1), *[("down", k) for k in range(last - LAG, last)], ("yT", 2 * NB - 1))
    return steps


TURNS = dict(xT=1, aqkv=3, asim=1, aT=1, aav=1, y=1, route=2, act=1, sbc=1, yT=1,
             bqkv=3, bs=1, bpT=1, bo=1, by=1)


def build(nc, x_d, small_d, gate_d, up_d, down_d, w2_d, cols_d, rows_d, out_d):
    steps = plan()
    turn_of = {}
    turns = 0
    for s in steps:
        if s[0] in TURNS:
            turn_of[s] = turns
            turns += TURNS[s[0]]
    xT_step = {(s[2], s[3]): s for s in steps if s[0] == "xT"}
    split_no = {s: i for i, s in enumerate(s for s in steps if s[0] == "xT" and s[2] != "A")}
    wrote = {("A", b): None for b in range(NB)}
    wrote |= {("F", b): ("y", b) for b in range(NB)} | {("B", b): ("yT", b) for b in range(NB)}
    wrote |= {("F", NB + b): ("by", b) for b in range(NB)}

    with ExitStack() as ctx:
        base = (nc.sbuf_base + 63) // 64 * 64
        cursor = [base]

        def sb(name, shape, dt=F32):
            size = 1
            for n in shape[1:]:
                size *= n
            size = (size * (2 if dt == BF16 else 4) + 31) // 32 * 32
            t = nc.alloc_sbuf_tensor_at(name, shape, dt, offset=cursor[0])
            cursor[0] += size
            return t

        X = sb("X", [P, NB * NT, D])
        WGh, WGl = (sb(n, [P, CH, P], F32R) for n in ("WGh", "WGl"))
        WUh, WUl = (sb(n, [P, CH, P], F32R) for n in ("WUh", "WUl"))
        WDh, WDl = (sb(n, [P, CH, P], F32R) for n in ("WDh", "WDl"))
        raw = sb("raw", [P, C_ALL])
        SWh, SWl = (sb(n, [P, C_ALL - C_BQKV], F32R) for n in ("SWh", "SWl"))
        ident = sb("ident", [P, P])
        w2 = sb("w2", [AH, KMAX + 2])
        cols = sb("cols", [P, 6])
        rows = sb("rows", [P, 272])
        bq = sb("bq", [P, 1])
        etemp = sb("etemp", [P, 1])
        ones = sb("ones", [P, P])
        hmask = sb("hmask", [P, P])
        nhalf = sb("nhalf", [P, NT])
        xhS, xlS = (sb(n, [P, T], F32R) for n in ("xhS", "xlS"))
        xhF = [sb(f"xhF{i}", [P, T], F32R) for i in range(2)]
        xlF = [sb(f"xlF{i}", [P, T], F32R) for i in range(2)]
        xn = sb("xn", [P, NT, D])
        bst = sb("bst", [P, NT, 6])
        mv = sb("mv", [P, NT, 2])
        rstd = sb("rstd", [P, NT])
        rt = sb("rt", [P, 3, NT])
        pe_ = sb("pe_", [P, NT, E])
        pr = sb("pr", [P, NT, E])
        p4 = sb("p4", [P, 6, NT])
        gt = sb("gt", [P, NT, E, E], BF16)
        ge = sb("ge", [P, NT, E, E], BF16)
        tri = sb("tri", [P, E, E], BF16)
        rk = sb("rk", [P, NT, E])
        al_ = sb("al_", [P, NT, KMAX])
        av_ = sb("av_", [P, NT, KMAX])
        kidx = sb("kidx", [P, NT, KMAX])
        sx = sb("sx", [P, NT, E, P // E])
        xa, hq = (sb(n, [AH, T]) for n in ("xa", "hq"))
        YT = sb("YT", [P, T])
        sbc = [sb(f"sbc{i}", [P, T]) for i in range(2)]
        sl = [sb(f"sl{i}", [P, T]) for i in range(2)]
        t2 = [sb(f"t2{i}", [P, T]) for i in range(3)]
        ah = [sb(f"ah{i}", [P, T], F32R) for i in range(2)]
        alo = [sb(f"alo{i}", [P, T], F32R) for i in range(2)]
        xaT = sb("xaT", [P, T])
        qk = sb("qk", [P, NT, 2, P])
        sq = sb("sq", [P, NT, 2, P])
        vT = sb("vT", [P, T])
        oA = sb("oA", [P, T])
        nss, nys, nts = (sb(n, [P, P + 1]) for n in ("nss", "nys", "nts"))
        sim, attn, attnT = (sb(n, [P, P]) for n in ("sim", "attn", "attnT"))
        amx, ars, ari = (sb(n, [P, 1]) for n in ("amx", "ars", "ari"))
        mark = cursor[0]
        stage = [sb(f"stage{i}", [P, WCOLS]) for i in range(NSTAGE)]
        end = cursor[0]
        cursor[0] = mark
        qF, kF = (sb(n, [P, T]) for n in ("qF", "kF"))
        qh, ql, kh, kl = (sb(n, [P, T], F32R) for n in ("qh", "ql", "kh", "kl"))
        vF = sb("vF", [P, NT, D])
        vh, vl = (sb(n, [P, NT, D], F32R) for n in ("vh", "vl"))
        Sb = sb("Sb", [P, NT, T])
        mk = [sb(f"mk{i}", [P, T], BF16) for i in range(4)]
        PTh, PTl = (sb(n, [P, NT, T], F32R) for n in ("PTh", "PTl"))
        oTh, oTl = (sb(n, [P, T], F32R) for n in ("oTh", "oTl"))
        bmx = sb("bmx", [P, NT])
        brs = sb("brs", [P, NT])
        bri = sb("bri", [P, NT])
        bt = sb("bt", [P, NT, D])
        cursor[0] = max(end, cursor[0])
        assert cursor[0] <= nc.sbuf_usable_end, cursor[0] - nc.sbuf_usable_end

        bank = [ctx.enter_context(nc.psum_tensor(f"bank{i}", [P, 512], F32)) for i in range(8)]
        OACC = bank[7]

        def sem(name):
            return ctx.enter_context(nc.semaphore(name))

        x_loaded = [sem(f"x_loaded{b}") for b in range(NB)]
        small_loaded = sem("small_loaded")
        rows_loaded = sem("rows_loaded")
        stage_loaded = [sem(f"stage_loaded{i}") for i in range(NSTAGE)]
        consts_ready = sem("consts_ready")
        pool_did = sem("pool_did")
        dve_did = sem("dve_did")
        dve_consts = sem("dve_consts")
        etemp_ready = sem("etemp_ready")
        bq_ready = sem("bq_ready")
        wn_ready = sem("wn_ready")
        swh_ready, swl_ready = sem("swh_ready"), sem("swl_ready")
        wh_ready, wl_dve, wl_pool = sem("wh_ready"), sem("wl_dve"), sem("wl_pool")
        stats_ready, rstd_ready, xn_ready, xh_ready = (sem(n) for n in ("stats_ready", "rstd_ready", "xn_ready", "xh_ready"))
        m_full = [sem(f"m_full{i}") for i in range(3)]
        m_free = [sem(f"m_free{i}") for i in range(3)]
        sq_ready, simx_ready, aexp_done, attn_ready = (
            sem(n) for n in ("sq_ready", "simx_ready", "aexp_done", "attn_ready"))
        exp8_ready, inner_ready, th_ready, g_ready, sx_ready = (
            sem(n) for n in ("exp8_ready", "inner_ready", "th_ready", "g_ready", "sx_ready"))
        pe_sub = sem("pe_sub")
        g_full, silu_done, u_full, t2_done, a_done = (sem(n) for n in ("g_full", "silu_done", "u_full", "t2_done", "a_done"))
        ahi_done, alo_done, down_done, y_free = (sem(n) for n in ("ahi_done", "alo_done", "down_done", "y_free"))
        qf_ready, qh_ready, qkl_ready, v_ready = (sem(n) for n in ("qf_ready", "qh_ready", "qkl_ready", "v_ready"))
        s_copied, sp_ready, bexp_done = sem("s_copied"), sem("sp_ready"), sem("bexp_done")
        pth_ready, oth_ready = sem("pth_ready"), sem("oth_ready")
        stored = sem("stored")

        def m_bank(t):
            return bank[4 + t % 3]

        def wait_full(eng, t):
            eng.wait_ge(m_full[t % 3], t // 3 + 1)

        def wait_free(eng, t):
            eng.wait_ge(m_free[t % 3], t // 3 + 1)

        def n_free(t):
            return m_free[t % 3]

        def last_turn(*step):
            return turn_of[step] + TURNS[step[0]] - 1

        def piece_of(j):
            hi, lo = ((WGh, WGl), (WUh, WUl), (WDh, WDl))[j % 3]
            at = slice(j // 3 * WCOLS, j // 3 * WCOLS + WCOLS)
            return (w[:, :, :].rearrange("p c n -> p (c n)")[:, at] for w in (hi, lo))

        block = ctx.enter_context(nc.Block())

        @block.sync
        def _(sp):
            xv = x_d.rearrange("b (i p) c -> p b i c", p=P)
            sp.dma_start(X[:, 0:NT, :], xv[:, 0]).then_inc(x_loaded[0], 16)
            sp.dma_start(raw[:, :], small_d).then_inc(small_loaded, 16)
            sp.dma_start(cols[:, :], cols_d).then_inc(small_loaded, 16)
            sp.dma_start(rows[:, :], rows_d.partition_broadcast(P)).then_inc(rows_loaded, 16)
            sp.dma_start(w2[:, 0:KMAX], w2_d).then_inc(small_loaded, 16)
            for s in steps:
                if s[0] == "wp":
                    j = s[1]
                    if j >= NSTAGE:
                        i = j - NSTAGE
                        sp.wait_ge(wl_pool if i % 3 == 2 else wl_dve, i // 3 + 1 if i % 3 == 2 else i // 3 * 2 + i % 3 + 1)
                    at = j // 3 * WCOLS
                    sp.dma_start(stage[j % NSTAGE][:, :], (gate_d, up_d, down_d)[j % 3][:, at:at + WCOLS])\
                      .then_inc(stage_loaded[j % NSTAGE], 16)
                    if 6 <= j < 6 + NB - 1:
                        b = j - 5
                        sp.dma_start(X[:, NT * b:NT * b + NT, :], xv[:, b]).then_inc(x_loaded[b], 16)
            for b in range(NB):
                wait_free(sp, turn_of["yT", NB + b])
                sp.dma_start(out_d.rearrange("b (i p) c -> p b i c", p=P)[:, b], X[:, NT * b:NT * b + NT, :])\
                  .then_inc(stored, 16)
            sp.wait_ge(stored, 16 * NB)

        @block.gpsimd
        def _(pool):
            did = [0]

            def chain(ins):
                did[0] += 1
                ins.then_inc(pool_did, 1)
                pool.wait_ge(pool_did, did[0])

            chain(pool.memset(ident[:, :], 0.0))
            chain(pool.affine_select(out=ident[:, :], in_=ident[:, :], compare_op=ALU.not_equal, fill=1.0,
                                     base=0, pattern=[[-1, P]], channel_multiplier=1))
            pool.memset(ones[:, :], 1.0)
            pool.memset(nhalf[:, :], -0.5).then_inc(consts_ready, 1)
            for e in range(H):
                own = hmask[:, e * DH:e * DH + DH]
                chain(pool.memset(own, 0.0))
                chain(pool.affine_select(out=own, in_=own, compare_op=ALU.is_ge, fill=NEG, base=-e * DH,
                                         pattern=[[0, DH]], channel_multiplier=1))
                r = pool.affine_select(out=own, in_=own, compare_op=ALU.is_ge, fill=NEG, base=e * DH + DH - 1,
                                       pattern=[[0, DH]], channel_multiplier=-1)
            r.then_inc(consts_ready, 1)

            for s in steps:
                kind = s[0]
                if kind == "stats":
                    _, seq, what, _b = s
                    if seq == 0:
                        pool.wait_ge(consts_ready, 1)
                    pool.wait_ge(stats_ready, seq + 1)
                    chain(pool.tensor_scalar(rt[:, 0], mv[:, :, 1], 1.0, LN_EPS, ALU.mult, ALU.add))
                    r = pool.tensor_tensor(rstd[:, :] if what != "A" else rt[:, 1], rt[:, 0], nhalf[:, :], ALU.pow)
                    if what == "A":
                        chain(r)
                        chain(pool.tensor_tensor(rt[:, 0], mv[:, :, 1], rt[:, 1], ALU.mult))
                        chain(pool.tensor_tensor(rt[:, 2], rt[:, 0], rt[:, 1], ALU.mult))
                        chain(pool.tensor_scalar(rt[:, 0], rt[:, 2], 1.0, RMS_EPS, ALU.mult, ALU.add))
                        chain(pool.tensor_tensor(rt[:, 2], rt[:, 0], nhalf[:, :], ALU.pow))
                        r = pool.tensor_tensor(rstd[:, :], rt[:, 1], rt[:, 2], ALU.mult)
                    r.then_inc(rstd_ready, 1)
                if kind == "aqkv":
                    b = s[1]
                    t = turn_of[s]
                    wait_free(pool, t)
                    wait_free(pool, t + 1)
                    if b:
                        wait_full(pool, turn_of["asim", b - 1])
                    pool.tensor_tensor(sq[:, :, :, :], qk[:, :, :, :], qk[:, :, :, :], ALU.mult).then_inc(sq_ready, 1)
                if kind == "wp" and s[1] % 3 == 2:
                    j = s[1]
                    pool.wait_ge(wh_ready, j + 1)
                    hi, lo = piece_of(j)
                    pool.tensor_tensor(lo, stage[j % NSTAGE][:, :], hi.bitcast(F32), ALU.subtract).then_inc(wl_pool, 1)
                if kind == "route":
                    n = s[1]
                    wait_free(pool, last_turn(*s))
                    chain(pool.tensor_scalar(hq[:, :], hq[:, :], 0.044715, 1.0, ALU.mult, ALU.add))
                    pool.tensor_tensor(hq[:, :], hq[:, :], xa[:, :], ALU.mult).then_inc(inner_ready, 1)
                if kind == "gu":
                    k = s[1]
                    pool.wait_ge(t2_done, k + 1)
                    pool.wait_ge(silu_done, k + 1)
                    pool.tensor_tensor(t2[k % 3][:, :], t2[k % 3][:, :], sl[k % 2][:, :], ALU.mult).then_inc(a_done, 1)

        @block.scalar
        def _(act):
            act.wait_ge(small_loaded, 48)
            act.activation(etemp[:, :], cols[:, 5:6], ACT.Exp).then_inc(etemp_ready, 1)
            act.activation(SWh[:, :], raw[:, C_BQKV:C_ALL], ACT.Copy).then_inc(swh_ready, 1)
            act.activation(bq[:, :], cols[:, 1:2], ACT.Copy, scale=B_SCALE).then_inc(bq_ready, 1)

            for s in steps:
                kind = s[0]
                if kind == "xT":
                    _, seq, what, b = s
                    t = turn_of[s]
                    wait_full(act, t)
                    if what == "A":
                        act.activation(xaT[:, :], m_bank(t)[:, :], ACT.Copy).then_inc(n_free(t), 1)
                        continue
                    if what == "F" and b >= 2:
                        act.wait_ge(u_full, CH * (b - 1))
                    if what == "B" and b:
                        wait_full(act, last_turn("bqkv", b - 1))
                    dst = xhF[b % 2] if what == "F" else xhS
                    act.activation(dst[:, :], m_bank(t)[:, :], ACT.Copy).then_inc(xh_ready, 1)
                if kind == "aqkv":
                    b = s[1]
                    t = turn_of[s]
                    if b:
                        wait_full(act, turn_of["asim", b - 1])
                        act.wait_ge(sq_ready, b)
                    for j in range(2):
                        wait_full(act, t + j)
                        act.activation(qk[:, 2 * j:2 * j + 2, :, :],
                                       m_bank(t + j)[:, :].rearrange("p (i r c) -> p i r c", i=2, r=2),
                                       ACT.Copy).then_inc(n_free(t + j), 1)
                    wait_full(act, t + 2)
                    if b:
                        wait_full(act, turn_of["aav", b - 1])
                    act.activation(vT[:, :], m_bank(t + 2)[:, :], ACT.Copy).then_inc(n_free(t + 2), 1)
                if kind == "aexp":
                    b = s[1]
                    act.wait_ge(simx_ready, b + 1)
                    act.activation(attn[:, :], sim[:, :], ACT.Exp, bias=amx[:, 0:1], accum_out=ars[:, 0:1])\
                       .then_inc(aexp_done, 1)
                if kind == "aT":
                    b = s[1]
                    t = turn_of[s]
                    wait_full(act, t)
                    act.activation(attnT[:, :], m_bank(t)[:, 0:P], ACT.Copy).then_inc(n_free(t), 1)
                if kind == "aav":
                    b = s[1]
                    t = turn_of[s]
                    wait_full(act, t)
                    if b:
                        wait_full(act, turn_of["y", b - 1])
                    act.activation(oA[:, :], m_bank(t)[:, :], ACT.Copy).then_inc(n_free(t), 1)
                if kind == "wp":
                    j = s[1]
                    act.wait_ge(stage_loaded[j % NSTAGE], 16 * (j // NSTAGE + 1))
                    hi, _lo = piece_of(j)
                    act.activation(hi, stage[j % NSTAGE][:, :], ACT.Copy).then_inc(wh_ready, 1)
                if kind == "route":
                    n = s[1]
                    t = turn_of[s]
                    act.wait_ge(pe_sub, n + 1)
                    act.activation(pe_[:, :, :], pe_[:, :, :], ACT.Exp).then_inc(exp8_ready, 1)
                    wait_full(act, t + 1)
                    if n:
                        wait_full(act, turn_of["act", n - 1])
                    act.activation(xa[:, :], m_bank(t + 1)[0:AH, :], ACT.Identity, bias=cols[0:AH, 4:5])
                    act.activation(hq[:, :], m_bank(t + 1)[0:AH, :], ACT.Square, bias=cols[0:AH, 4:5])\
                       .then_inc(n_free(t + 1), 1)
                if kind == "gelu":
                    n = s[1]
                    act.wait_ge(inner_ready, n + 1)
                    act.activation(hq[:, :], hq[:, :], ACT.Tanh, scale=0.7978845608028654).then_inc(th_ready, 1)
                if kind == "sbc":
                    n = s[1]
                    t = turn_of[s]
                    wait_full(act, t)
                    if n >= 2:
                        act.wait_ge(t2_done, CH * (n - 1))
                    act.activation(sbc[n % 2][:, :], m_bank(t)[:, :], ACT.Copy).then_inc(n_free(t), 1)
                if kind == "gu":
                    k = s[1]
                    act.wait_ge(g_full, k + 1)
                    if k >= 2:
                        act.wait_ge(a_done, k - 1)
                    act.activation(sl[k % 2][:, :], bank[k % 2][:, :], ACT.Silu).then_inc(silu_done, 1)
                if kind == "hl":
                    k = s[1]
                    act.wait_ge(a_done, k + 1)
                    if k >= 2:
                        act.wait_ge(down_done, k - 1)
                    act.activation(ah[k % 2][:, :], t2[k % 3][:, :], ACT.Copy).then_inc(ahi_done, 1)
                if kind == "down" and s[1] % CH == CH - 1:
                    n = s[1] // CH
                    act.wait_ge(down_done, CH * (n + 1))
                    if n:
                        wait_full(act, turn_of["yT", n - 1])
                    act.activation(YT[:, :], OACC[:, :], ACT.Copy).then_inc(y_free, 1)
                if kind == "bqkv":
                    b = s[1]
                    t = turn_of[s]
                    if b == 0:
                        act.wait_ge(bq_ready, 1)
                    else:
                        wait_full(act, turn_of["bs", b - 1, NT - 1])
                        act.wait_ge(qkl_ready, b)
                    wait_full(act, t)
                    act.activation(qF[:, :], m_bank(t)[:, :], ACT.Identity, bias=bq[:, 0:1], scale=B_SCALE).then_inc(qf_ready, 1)
                    act.wait_ge(qf_ready, 2 * b + 1)
                    act.activation(qh[:, :], qF[:, :], ACT.Copy).then_inc(n_free(t), 1)
                    wait_full(act, t + 1)
                    act.activation(kF[:, :], m_bank(t + 1)[:, :], ACT.Identity, bias=cols[:, 2:3]).then_inc(qf_ready, 1)
                    act.wait_ge(qf_ready, 2 * b + 2)
                    act.activation(kh[:, :], kF[:, :], ACT.Copy).then_inc(n_free(t + 1), 1)
                if kind == "bs":
                    _, b, i = s
                    t = turn_of[s]
                    wait_full(act, t)
                    if b:
                        wait_full(act, turn_of["bpT", b - 1, NT - 1])
                    act.activation(Sb[:, i, :], m_bank(t)[:, :], ACT.Copy).then_inc(n_free(t), 1)
                if kind == "bexp":
                    b = s[1]
                    for i in range(NT):
                        act.wait_ge(sp_ready, NT * b + i + 1)
                        act.activation(Sb[:, i, :], Sb[:, i, :], ACT.Exp, bias=bmx[:, i:i + 1],
                                       accum_out=brs[:, i:i + 1]).then_inc(bexp_done, 1)
                if kind == "bpT":
                    _, b, j = s
                    t = turn_of[s]
                    wait_full(act, t)
                    if b:
                        wait_full(act, turn_of["bo", b - 1])
                    act.activation(PTh[:, j, :], m_bank(t)[:, :], ACT.Copy).then_inc(pth_ready, 1)
                if kind == "bo":
                    b = s[1]
                    t = turn_of[s]
                    wait_full(act, t)
                    if b:
                        wait_full(act, turn_of["by", b - 1])
                    act.activation(oTh[:, :], m_bank(t)[:, :], ACT.Copy).then_inc(oth_ready, 1)

        @block.vector
        def _(dve):
            did = [0]

            def chain(ins):
                did[0] += 1
                ins.then_inc(dve_did, 1)
                dve.wait_ge(dve_did, did[0])

            for e in range(E):
                if e:
                    dve.memset(tri[:, e, 0:e], 1.0)
                dve.memset(tri[:, e, e:E], 0.0)
            for j in range(KMAX):
                r = dve.memset(kidx[:, :, j:j + 1], float(j + 1))
            chain(r)
            dve.wait_ge(small_loaded, 48)
            dve.tensor_scalar(raw[:, 0:384], raw[:, 0:384], cols[:, 0:1], None, ALU.mult).then_inc(wn_ready, 1)
            dve.wait_ge(wn_ready, 1)
            dve.wait_ge(swh_ready, 1)
            dve.tensor_tensor(SWl[:, :], raw[:, C_BQKV:C_ALL], SWh[:, :].bitcast(F32), ALU.subtract).then_inc(swl_ready, 1)

            for s in steps:
                kind = s[0]
                if kind == "stats":
                    _, seq, what, b = s
                    q = b % NB
                    src = wrote[what, b]
                    if src is None:
                        dve.wait_ge(x_loaded[q], 16)
                    else:
                        wait_free(dve, turn_of[src])
                    for i in range(NT):
                        r = dve.bn_stats(bst[:, i, :], X[:, NT * q + i, :])
                    chain(r)
                    for i in range(NT):
                        r = dve.bn_aggr(mv[:, i, :], bst[:, i, :])
                    r.then_inc(stats_ready, 1)
                if kind == "xn":
                    _, seq, what, b = s
                    q = b % NB
                    dve.wait_ge(rstd_ready, seq + 1)
                    for i in range(NT):
                        r = dve.tensor_scalar(xn[:, i, :], X[:, NT * q + i, :], mv[:, i, 0:1], rstd[:, i:i + 1],
                                              ALU.subtract, ALU.mult)
                    r.then_inc(xn_ready, 1)
                if kind == "xT":
                    _, seq, what, b = s
                    t = turn_of[s]
                    if what == "A":
                        continue
                    dst, hi = (xlF[b % 2], xhF[b % 2]) if what == "F" else (xlS, xhS)
                    dve.wait_ge(xh_ready, split_no[s] + 1)
                    if what == "B" and b:
                        wait_full(dve, last_turn("bqkv", b - 1))
                    dve.tensor_tensor(dst[:, :], m_bank(t)[:, :], hi[:, :].bitcast(F32), ALU.subtract).then_inc(n_free(t), 1)
                if kind == "wp" and s[1] % 3 != 2:
                    j = s[1]
                    dve.wait_ge(wh_ready, j + 1)
                    hi, lo = piece_of(j)
                    dve.tensor_tensor(lo, stage[j % NSTAGE][:, :], hi.bitcast(F32), ALU.subtract).then_inc(wl_dve, 1)
                if kind == "asim":
                    b = s[1]
                    t = turn_of[s]
                    m = m_bank(t)
                    wait_full(dve, t)
                    chain(dve.tensor_scalar(nss[:, :], m[:, P:2 * P + 1], 1e-24, None, ALU.max))
                    chain(dve.tensor_scalar(nys[:, :].bitcast(I32), nss[:, :].bitcast(I32), -0.5, RSQRT_SEED,
                                            ALU.mult, ALU.add))
                    for _ in range(3):
                        chain(dve.tensor_tensor(nts[:, :], nys[:, :], nys[:, :], ALU.mult))
                        chain(dve.scalar_tensor_tensor(nts[:, :], nts[:, :], -0.5, nss[:, :], ALU.mult, ALU.mult))
                        chain(dve.scalar_tensor_tensor(nys[:, :], nts[:, :], 1.5, nys[:, :], ALU.add, ALU.mult))
                    if b == 0:
                        dve.wait_ge(etemp_ready, 1)
                        dve.wait_ge(consts_ready, 2)
                    chain(dve.tensor_tensor(nts[:, P:P + 1], nys[:, P:P + 1], etemp[:, 0:1], ALU.mult))
                    if b:
                        dve.wait_ge(aexp_done, b)
                    dve.scalar_tensor_tensor(sim[:, :], m[:, 0:P], nts[:, P:P + 1], nys[:, 0:P], ALU.mult, ALU.mult)\
                       .then_inc(n_free(t), 1)
                    wait_free(dve, t)
                    chain(dve.tensor_tensor(sim[:, :], sim[:, :], hmask[:, :], ALU.add))
                    dve.tensor_reduce(amx[:, 0:1], sim[:, :], AX_X, ALU.max, negate=True).then_inc(simx_ready, 1)
                if kind == "aT":
                    b = s[1]
                    dve.wait_ge(aexp_done, b + 1)
                    chain(dve.reciprocal(ari[:, :], ars[:, :]))
                    dve.tensor_scalar(attn[:, :], attn[:, :], ari[:, 0:1], None, ALU.mult).then_inc(attn_ready, 1)
                if kind in ("y", "yT"):
                    t = turn_of[s]
                    q = s[1] % NB
                    wait_full(dve, t)
                    xs = X[:, NT * q:NT * q + NT, :].rearrange("p i d -> p (i d)")
                    dve.tensor_tensor(xs, m_bank(t)[:, :], xs, ALU.add).then_inc(n_free(t), 1)
                if kind == "route":
                    n = s[1]
                    t = turn_of[s]
                    wait_full(dve, t)
                    lg = m_bank(t)[:, 0:NT * E].rearrange("p (i e) -> p i e", e=E)
                    chain(dve.tensor_reduce(p4[:, 0], lg, AX_X, ALU.max))
                    dve.tensor_tensor(pe_[:, :, :], lg, p4[:, 0].unsqueeze(2).to_broadcast([P, NT, E]),
                                      ALU.subtract).then_inc(pe_sub, 1)
                    dve.wait_ge(pe_sub, n + 1)
                    dve.tensor_copy(p4[:, 5], p4[:, 0]).then_inc(n_free(t), 1)
                if kind == "gelu":
                    n = s[1]
                    dve.wait_ge(exp8_ready, n + 1)
                    chain(dve.tensor_reduce(p4[:, 1], pe_[:, :, :], AX_X, ALU.add))
                    chain(dve.reciprocal(p4[:, 2], p4[:, 1]))
                    chain(dve.tensor_tensor(pr[:, :, :], pe_[:, :, :], p4[:, 2].unsqueeze(2).to_broadcast([P, NT, E]), ALU.mult))
                    other = pr[:, :, :].unsqueeze(2).to_broadcast([P, NT, E, E])
                    own = pr[:, :, :].unsqueeze(3).to_broadcast([P, NT, E, E])
                    dve.tensor_tensor(gt[:, :, :, :], other, own, ALU.is_gt)
                    chain(dve.tensor_tensor(ge[:, :, :, :], other, own, ALU.is_ge))
                    chain(dve.tensor_tensor(ge[:, :, :, :], ge[:, :, :, :],
                                            tri[:, :, :].unsqueeze(1).to_broadcast([P, NT, E, E]), ALU.mult))
                    chain(dve.tensor_tensor(gt[:, :, :, :], gt[:, :, :, :], ge[:, :, :, :], ALU.max))
                    chain(dve.tensor_reduce(rk[:, :, :], gt[:, :, :, :], AX_X, ALU.add))
                    dve.wait_ge(th_ready, n + 1)
                    dve.scalar_tensor_tensor(hq[:, :], hq[:, :], 1.0, xa[:, :], ALU.add, ALU.mult).then_inc(g_ready, 1)
                if kind == "act":
                    n = s[1]
                    t = turn_of[s]
                    if n == 0:
                        dve.wait_ge(rows_loaded, 16)
                    wait_full(dve, t)
                    lg = m_bank(t)[:, 0:NT * 8].rearrange("p (i e) -> p i e", e=8)[:, :, 0:KMAX]
                    dve.scalar_tensor_tensor(al_[:, :, :], lg, 0.5,
                                             rows[:, 256:262].unsqueeze(1).to_broadcast([P, NT, KMAX]),
                                             ALU.mult, ALU.add).then_inc(n_free(t), 1)
                    wait_free(dve, t)
                    chain(dve.tensor_scalar(al_[:, :, :], al_[:, :, :], 30.0, -30.0, ALU.min, ALU.max))
                    chain(dve.tensor_reduce(p4[:, 3], al_[:, :, :], AX_X, ALU.max))
                    chain(dve.tensor_tensor(av_[:, :, :], al_[:, :, :], p4[:, 3].unsqueeze(2).to_broadcast([P, NT, KMAX]), ALU.is_ge))
                    chain(dve.scalar_tensor_tensor(av_[:, :, :], av_[:, :, :], -16.0, kidx[:, :, :], ALU.mult, ALU.add))
                    chain(dve.tensor_reduce(p4[:, 4], av_[:, :, :], AX_X, ALU.min))
                    chain(dve.scalar_tensor_tensor(rk[:, :, :], rk[:, :, :], -16.0,
                                                   p4[:, 4].unsqueeze(2).to_broadcast([P, NT, E]), ALU.add, ALU.is_lt))
                    if n:
                        wait_full(dve, turn_of["sbc", n - 1])
                    dve.tensor_tensor(sx[:, :, :, :], rk[:, :, :].unsqueeze(3).to_broadcast([P, NT, E, P // E]),
                                      pr[:, :, :].unsqueeze(3).to_broadcast([P, NT, E, P // E]), ALU.mult).then_inc(sx_ready, 1)
                if kind == "gu":
                    k = s[1]
                    if k % CH == 0:
                        wait_free(dve, turn_of["sbc", k // CH])
                    dve.wait_ge(u_full, k + 1)
                    if k >= 3:
                        dve.wait_ge(alo_done, k - 2)
                    dve.tensor_tensor(t2[k % 3][:, :], bank[2 + k % 2][:, :], sbc[k // CH % 2][:, :],
                                      ALU.mult).then_inc(t2_done, 1)
                if kind == "hl":
                    k = s[1]
                    dve.wait_ge(ahi_done, k + 1)
                    if k >= 2:
                        dve.wait_ge(down_done, k - 1)
                    dve.tensor_tensor(alo[k % 2][:, :], t2[k % 3][:, :], ah[k % 2][:, :].bitcast(F32),
                                      ALU.subtract).then_inc(alo_done, 1)
                if kind == "bqkv":
                    b = s[1]
                    t = turn_of[s]
                    wait_free(dve, t)
                    dve.tensor_tensor(ql[:, :], qF[:, :], qh[:, :].bitcast(F32), ALU.subtract)
                    wait_free(dve, t + 1)
                    dve.tensor_tensor(kl[:, :], kF[:, :], kh[:, :].bitcast(F32), ALU.subtract).then_inc(qkl_ready, 1)
                    wait_full(dve, t + 2)
                    dve.tensor_tensor(vF[:, :, :], m_bank(t + 2)[:, :].rearrange("p (i d) -> p i d", d=D),
                                      rows[:, 0:P].unsqueeze(1).to_broadcast([P, NT, D]), ALU.add).then_inc(n_free(t + 2), 1)
                    wait_free(dve, t + 2)
                    chain(dve.tensor_copy(vh[:, :, :], vF[:, :, :]))
                    dve.tensor_tensor(vl[:, :, :], vF[:, :, :], vh[:, :, :].bitcast(F32), ALU.subtract).then_inc(v_ready, 1)
                if kind == "bsp":
                    _, b, i = s
                    wait_free(dve, turn_of["bs", b, i])
                    x_ = Sb[:, i, :]
                    for m, (c, op, w) in zip(mk, ((X10, ALU.is_ge, 2.0), (X25, ALU.is_ge, 7.0),
                                                  (X85, ALU.is_gt, 5.0), (X95, ALU.is_gt, 5.0))):
                        r = dve.tensor_scalar(m[:, :], x_, c, w, op, ALU.mult)
                    chain(r)
                    dve.tensor_tensor(mk[0][:, :], mk[0][:, :], mk[1][:, :], ALU.add)
                    chain(dve.tensor_tensor(mk[2][:, :], mk[2][:, :], mk[3][:, :], ALU.add))
                    chain(dve.tensor_tensor(mk[0][:, :], mk[0][:, :], mk[2][:, :], ALU.add))
                    chain(dve.tensor_scalar(mk[1][:, :], mk[0][:, :], 1.0, None, ALU.add))
                    chain(dve.scalar_tensor_tensor(Sb[:, i, :], mk[1][:, :], 0.1, x_, ALU.mult, ALU.mult))
                    dve.tensor_reduce(bmx[:, i:i + 1], Sb[:, i, :], AX_X, ALU.max, negate=True).then_inc(sp_ready, 1)
                if kind == "bpT":
                    _, b, j = s
                    t = turn_of[s]
                    if j == 0:
                        dve.wait_ge(bexp_done, NT * (b + 1))
                        dve.reciprocal(bri[:, :], brs[:, :])
                    dve.wait_ge(pth_ready, NT * b + j + 1)
                    dve.tensor_tensor(PTl[:, j, :], m_bank(t)[:, :], PTh[:, j, :].bitcast(F32), ALU.subtract).then_inc(n_free(t), 1)
                if kind == "bo":
                    b = s[1]
                    t = turn_of[s]
                    dve.wait_ge(oth_ready, b + 1)
                    dve.tensor_tensor(oTl[:, :], m_bank(t)[:, :], oTh[:, :].bitcast(F32), ALU.subtract).then_inc(n_free(t), 1)
                if kind == "by":
                    b = s[1]
                    t = turn_of[s]
                    wait_full(dve, t)
                    for i in range(NT):
                        r = dve.scalar_tensor_tensor(bt[:, i, :], m_bank(t)[:, i * P:i * P + P], bri[:, i:i + 1],
                                                     rows[:, P:2 * P], ALU.mult, ALU.add)
                    chain(r)
                    xs = X[:, NT * b:NT * b + NT, :]
                    dve.tensor_tensor(xs, xs, bt[:, :, :], ALU.add).then_inc(n_free(t), 1)

        @block.tensor
        def _(pe):
            def turn(t):
                if t >= 3:
                    wait_free(pe, t - 3)
                return m_bank(t)

            def three(out, lh, ll, rh, rl, start=True, stop=True):
                pe.matmul(out, lh, rh, start=start, stop=False)
                pe.matmul(out, lh, rl, start=False, stop=False)
                return pe.matmul(out, ll, rh, start=False, stop=stop)

            def swide(c, n):
                return SWh[:, c - C_BQKV:c - C_BQKV + n], SWl[:, c - C_BQKV:c - C_BQKV + n]

            pe.wait_ge(consts_ready, 1)
            for s in steps:
                kind = s[0]
                if kind == "xT":
                    _, seq, what, b = s
                    t = turn_of[s]
                    pe.wait_ge(xn_ready, seq + 1)
                    m = turn(t)
                    for i in range(NT):
                        r = pe.transpose(m[:, i * P:i * P + P], xn[:, i, :], ident[:, :])
                    r.then_inc(m_full[t % 3], 1)
                if kind == "aqkv":
                    b = s[1]
                    t = turn_of[s]
                    if b == 0:
                        pe.wait_ge(wn_ready, 1)
                    wait_free(pe, turn_of[xT_step["A", b]])
                    for j in range(2):
                        m = turn(t + j)
                        for i in range(2):
                            r = pe.matmul(m[:, 256 * i:256 * i + 256], xaT[:, (2 * j + i) * P:(2 * j + i) * P + P],
                                          raw[:, C_QKV:C_QKV + 256], start=True, stop=True)
                        r.then_inc(m_full[(t + j) % 3], 1)
                    pe.matmul(turn(t + 2)[:, :], raw[:, C_QKV + 256:C_QKV + 384], xaT[:, :], start=True, stop=True)\
                      .then_inc(m_full[(t + 2) % 3], 1)
                if kind == "asim":
                    b = s[1]
                    t = turn_of[s]
                    m = turn(t)
                    wait_free(pe, turn_of["aqkv", b])
                    wait_free(pe, turn_of["aqkv", b] + 1)
                    for i in range(NT):
                        pe.matmul(m[:, 0:P], qk[:, i, 0, :], qk[:, i, 1, :], start=(i == 0), stop=(i == NT - 1))
                    pe.wait_ge(sq_ready, b + 1)
                    if b == 0:
                        pe.wait_ge(consts_ready, 2)
                    for i in range(NT):
                        pe.matmul(m[:, P:2 * P], ones[:, :], sq[:, i, 1, :], start=(i == 0), stop=(i == NT - 1))
                    for i in range(NT):
                        r = pe.matmul(m[:, 2 * P:2 * P + 1], sq[:, i, 0, :], ones[:, 0:1], start=(i == 0), stop=(i == NT - 1))
                    r.then_inc(m_full[t % 3], 1)
                if kind == "aT":
                    b = s[1]
                    t = turn_of[s]
                    pe.wait_ge(attn_ready, b + 1)
                    pe.transpose(turn(t)[:, 0:P], attn[:, :], ident[:, :]).then_inc(m_full[t % 3], 1)
                if kind == "aav":
                    b = s[1]
                    t = turn_of[s]
                    wait_free(pe, turn_of["aT", b])
                    pe.matmul(turn(t)[:, :], attnT[:, :], vT[:, :], start=True, stop=True).then_inc(m_full[t % 3], 1)
                if kind == "y":
                    b = s[1]
                    t = turn_of[s]
                    wait_free(pe, turn_of["aav", b])
                    m = turn(t)
                    for i in range(NT):
                        a = slice(i * P, i * P + P)
                        r = pe.matmul(m[:, a], oA[:, a], raw[:, C_OUT:C_OUT + P], start=True, stop=True)
                    r.then_inc(m_full[t % 3], 1)
                if kind == "route":
                    n = s[1]
                    t = turn_of[s]
                    if n == 0:
                        pe.wait_ge(swl_ready, 1)
                    wait_free(pe, turn_of[xT_step["F", n]])
                    xh, xl = xhF[n % 2], xlF[n % 2]
                    m = turn(t)
                    wh, wl = swide(C_ROUTER, E)
                    for i in range(NT):
                        a = slice(i * P, i * P + P)
                        r = three(m[:, i * E:i * E + E], xh[:, a], xl[:, a], wh, wl)
                    r.then_inc(m_full[t % 3], 1)
                    m = turn(t + 1)
                    wh, wl = swide(C_ACTOR, P)
                    three(m[:, :], wh, wl, xh[:, :], xl[:, :]).then_inc(m_full[(t + 1) % 3], 1)
                if kind == "act":
                    n = s[1]
                    t = turn_of[s]
                    pe.wait_ge(g_ready, n + 1)
                    m = turn(t)
                    for i in range(NT):
                        r = pe.matmul(m[:, 8 * i:8 * i + KMAX], hq[:, i * P:i * P + P], w2[:, 0:KMAX], start=True, stop=True)
                    r.then_inc(m_full[t % 3], 1)
                if kind == "sbc":
                    n = s[1]
                    t = turn_of[s]
                    pe.wait_ge(sx_ready, n + 1)
                    m = turn(t)
                    for i in range(NT):
                        r = pe.transpose(m[:, i * P:i * P + P], sx[:, i, :, :].rearrange("p e r -> p (e r)"), ident[:, :])
                    r.then_inc(m_full[t % 3], 1)
                if kind == "gu":
                    k = s[1]
                    n, c = k // CH, k % CH
                    if k < CH and c % WCH == 0:
                        pe.wait_ge(wl_dve, 2 * (c // WCH) + 2)
                    if c == 0:
                        wait_free(pe, turn_of[xT_step["F", n]])
                    xh, xl = xhF[n % 2][:, :], xlF[n % 2][:, :]
                    if k >= 2:
                        pe.wait_ge(silu_done, k - 1)
                    three(bank[k % 2][:, :], WGh[:, c, :], WGl[:, c, :], xh, xl).then_inc(g_full, 1)
                    if k >= 2:
                        pe.wait_ge(t2_done, k - 1)
                    three(bank[2 + k % 2][:, :], WUh[:, c, :], WUl[:, c, :], xh, xl).then_inc(u_full, 1)
                if kind == "down":
                    k = s[1]
                    n, c = k // CH, k % CH
                    pe.wait_ge(alo_done, k + 1)
                    if k < CH and c % WCH == 0:
                        pe.wait_ge(wl_pool, c // WCH + 1)
                    if n and c == 0:
                        pe.wait_ge(y_free, n)
                    three(OACC[:, :], WDh[:, c, :], WDl[:, c, :], ah[k % 2][:, :], alo[k % 2][:, :],
                          start=(c == 0), stop=(c == CH - 1)).then_inc(down_done, 1)
                if kind == "yT":
                    n = s[1]
                    t = turn_of[s]
                    pe.wait_ge(y_free, n + 1)
                    m = turn(t)
                    for i in range(NT):
                        r = pe.transpose(m[:, i * P:i * P + P], YT[:, i * P:i * P + P], ident[:, :])
                    r.then_inc(m_full[t % 3], 1)
                if kind == "bqkv":
                    b = s[1]
                    t = turn_of[s]
                    wait_free(pe, turn_of[xT_step["B", b]])
                    for j in range(2):
                        wh, wl = swide(C_BQKV + P * j, P)
                        three(turn(t + j)[:, :], wh, wl, xhS[:, :], xlS[:, :]).then_inc(m_full[(t + j) % 3], 1)
                    wh, wl = swide(C_BQKV + 2 * P, P)
                    m = turn(t + 2)
                    for i in range(NT):
                        a = slice(i * P, i * P + P)
                        r = three(m[:, a], xhS[:, a], xlS[:, a], wh, wl)
                    r.then_inc(m_full[(t + 2) % 3], 1)
                if kind == "bs":
                    _, b, i = s
                    t = turn_of[s]
                    pe.wait_ge(qkl_ready, b + 1)
                    a = slice(i * P, i * P + P)
                    three(turn(t)[:, :], qh[:, a], ql[:, a], kh[:, :], kl[:, :]).then_inc(m_full[t % 3], 1)
                if kind == "bpT":
                    _, b, j = s
                    t = turn_of[s]
                    pe.wait_ge(bexp_done, NT * (b + 1))
                    m = turn(t)
                    for i in range(NT):
                        r = pe.transpose(m[:, i * P:i * P + P], Sb[:, i, j * P:j * P + P], ident[:, :])
                    r.then_inc(m_full[t % 3], 1)
                if kind == "bo":
                    b = s[1]
                    t = turn_of[s]
                    pe.wait_ge(v_ready, b + 1)
                    m = turn(t)
                    for j in range(NT):
                        wait_free(pe, turn_of["bpT", b, j])
                        r = three(m[:, :], vh[:, j, :], vl[:, j, :], PTh[:, j, :], PTl[:, j, :],
                                  start=(j == 0), stop=(j == NT - 1))
                    r.then_inc(m_full[t % 3], 1)
                if kind == "by":
                    b = s[1]
                    t = turn_of[s]
                    wait_free(pe, turn_of["bo", b])
                    m = turn(t)
                    wh, wl = swide(C_BPROJ, P)
                    for i in range(NT):
                        a = slice(i * P, i * P + P)
                        r = three(m[:, a], oTh[:, a], oTl[:, a], wh, wl)
                    r.then_inc(m_full[t % 3], 1)


def kernel(L0_attn_a_x, L0_attn_a_norm_weight, L0_attn_a_w_qkv, L0_attn_a_temperature, L0_attn_a_w_out,
           L0_attn_b_W_qkv, L0_attn_b_b_qkv, L0_attn_b_W_proj, L0_attn_b_b_proj, L0_ffn_router_w,
           L0_ffn_actor_w1, L0_ffn_actor_b1, L0_ffn_actor_w2, L0_ffn_actor_b2, L0_ffn_gate_w, L0_ffn_up_w,
           L0_ffn_down_w):
    import numpy as np
    import concourse.bacc as bacc
    from concourse.bass_utils import run_bass_kernel_spmd

    a = lambda v: np.asarray(v)
    small = np.zeros((P, C_ALL), np.float32)
    small[:, C_QKV:C_QKV + 384] = a(L0_attn_a_w_qkv).T
    small[:, C_OUT:C_OUT + P] = a(L0_attn_a_w_out).T
    small[:, C_BQKV:C_BQKV + 384] = a(L0_attn_b_W_qkv)
    small[:, C_BPROJ:C_BPROJ + P] = a(L0_attn_b_W_proj)
    small[:, C_ROUTER:C_ROUTER + E] = a(L0_ffn_router_w).T
    small[:, C_ACTOR:C_ACTOR + AH] = a(L0_ffn_actor_w1).T
    columns = np.zeros((P, 6), np.float32)
    columns[:, 0] = a(L0_attn_a_norm_weight)
    columns[:, 1:4] = a(L0_attn_b_b_qkv).reshape(3, P).T
    columns[:AH, 4] = a(L0_ffn_actor_b1)
    columns[:, 5] = np.repeat(a(L0_attn_a_temperature).reshape(H), DH)
    row = np.zeros((272,), np.float32)
    row[0:P] = a(L0_attn_b_b_qkv)[2 * P:]
    row[P:2 * P] = a(L0_attn_b_b_proj)
    row[256:262] = a(L0_ffn_actor_b2)

    def hidden_cols(w):
        return np.ascontiguousarray(a(w).reshape(E, CH, 16, D).transpose(3, 1, 0, 2).reshape(D, CH * P))

    arrays = {
        "x": np.ascontiguousarray(a(L0_attn_a_x)),
        "small": small,
        "gate": hidden_cols(L0_ffn_gate_w),
        "up": hidden_cols(L0_ffn_up_w),
        "down": np.ascontiguousarray(a(L0_ffn_down_w).reshape(E, D, CH, 16).transpose(0, 3, 2, 1).reshape(P, CH * D)),
        "w2": np.ascontiguousarray(a(L0_ffn_actor_w2).T),
        "columns": columns,
        "row": row,
    }
    nc = bacc.Bacc("TRN2", target_bir_lowering=False, num_devices=1)
    args = [nc.dram_tensor(f"in_{n}", v.shape, F32, kind="ExternalInput").ap() for n, v in arrays.items()]
    args.append(nc.dram_tensor("out", arrays["x"].shape, F32, kind="ExternalOutput").ap())
    build(nc, *args)
    r = run_bass_kernel_spmd(nc, [{f"in_{n}": v for n, v in arrays.items()}], core_ids=[0])
    return r.results[0]["out"]
```

```python
from contextlib import ExitStack

import concourse.bass as bass
from concourse import mybir

F32 = mybir.dt.float32
F32R = mybir.dt.float32r
BF16 = mybir.dt.bfloat16
ALU = mybir.AluOpType
ACT = mybir.ActivationFunctionType
AX_X = mybir.AxisListType.X

P = 128
NB = 4
T = 512
NT = T // P
D = 128
H, DH = 8, 16
E, I, CH = 8, 336, 21
KMAX, AH = 6, 50
LN_EPS, RMS_EPS = 1e-5, 1e-6
B_SCALE = 8 ** -0.5 / 10
X10, X25, X85, X95 = (-2.1972245773362196, -1.0986122886681098, 1.7346010553881064, 2.9444389791664403)
LAG = 3
WCH = 3
WCOLS = WCH * P
NSTAGE = 6
NEG = -1e30

C_QKV, C_OUT, C_BQKV, C_BPROJ, C_ROUTER, C_ACTOR = 0, 384, 512, 896, 1024, 1032
C_ALL = C_ACTOR + P


A_STEPS = [(0, "stats"), (1, "xn"), (3, "xT"), (5, "aqk", 0), (6, "aqk", 1), (8, "av"), (9, "asim"), (10, "ass"),
           (11, "ascale"), (13, "asT"), (14, "amax"), (15, "aexp"), (17, "aT"), (19, "aav"), (21, "y")]
BEXP_AT = ((19, 0), (19, 1), (27, 2), (27, 3))
B_STEPS = ([(0, "stats"), (1, "xn"), (3, "xT"), (4, "xl"), (6, "bqk", 0), (7, "bqk", 1), (7, "bqkl", 0), (8, "bqkl", 1)]
           + [(10 + 4 * i, "bs", i) for i in range(NT)]
           + [(11 + 4 * i + part, "bsp", i, part) for i in range(NT) for part in range(4)]
           + [(15, "bv"), (17, "bvl"), *[(at, "bexp", i) for at, i in BEXP_AT]]
           + [(30 + j, "bpl", j) for j in range(NT)] + [(29 + j, "bpT", j) for j in range(NT)]
           + [(32, "bo", 0), (34, "bo", 1), (35, "bol"), (37, "by"), (38, "byx")])
B_EVERY = 21
A_STARTS = (-42, -30, 0, 18)
F_STEPS = [(0, "stats"), (1, "xn"), (3, "xT"), (4, "xl"), (6, "route"), (7, "rexp"), (7, "inner", 0), (8, "inner", 1),
           (9, "rsum"), (10, "rrank"), (10, "tanh"), (11, "gelu"), (13, "act"), (14, "actk"), (16, "sbc")]
GU_AFTER = {("tanh", 0): 0, ("act", 0): 1}
SHIFTS = 1
F_AHEAD = 21


TURNS = dict(xT=1, aqk=1, av=1, asim=1, asT=1, aT=1, aav=1, y=1, route=2, act=1, sbc=1, yT=1,
             bqk=1, bv=1, bs=1, bpT=1, bo=1, by=1)

FREED_BY = dict(asim="ascale", asT="amax", act="actk", bpT="bpl", bo="bol", by="byx")
COST = dict(stats=(0, 0, 1.2), xn=(0, 0, 1.1), xT=(.4, .5, 0), xl=(0, 0, .6), aqk=(.9, 1, 0), av=(.9, .5, 0),
            asim=(1.3, 0, 0), ass=(0, 0, .1), ascale=(0, 0, .3), asT=(.1, 0, 0), amax=(0, 0, .5), aexp=(0, 3, 0),
            aT=(.1, .2, .1), aav=(.9, .5, 0), y=(.9, 0, .6), route=(2, 1.1, .3), rexp=(0, 2.7, 0),
            rsum=(0, 0, 1.3), rrank=(0, 0, 1.1), tanh=(0, .5, 0), gelu=(0, 0, .6), act=(.9, 0, 0), actk=(0, 0, 1.9),
            sbc=(.4, .5, 0), yT=(.4, 0, .6), bqk=(.7, 1, 0), bqkl=(0, 0, .6), bs=(.7, .5, 0), bsp=(0, 0, .9),
            bv=(.7, 0, .6), bvl=(0, 0, 1), bexp=(0, 1.2, 0), bpT=(.4, .5, 0), bpl=(0, 0, .6), bo=(1.3, .3, 0),
            bol=(0, 0, .6), by=(.7, 0, 0), byx=(0, 0, 1.4))
DEBT = 1.0


def thread(kind, b, steps, start):
    norm = ("stats", "xn", "xT", "xl")
    return [start, [(s[0], (s[1], kind, b) if s[1] in norm else (s[1], b) + s[2:])
                    for s in sorted(steps, key=lambda v: v[0])], 0]


def needs(s):
    kind, b = s[0], s[-1] if s[0] in ("stats", "xn", "xT", "xl") else s[1]
    prev = b - 1
    if kind == "stats":
        return {"A": [], "F": [("y", b) if b < NB else ("byx", b - NB)], "B": [("yT", b)]}[s[1]]
    if kind == "xT" and s[1] == "A":
        return [("av", prev)]
    if kind in ("xT", "xl") and s[1] == "B":
        return [("bv", prev)]
    if kind == "yT":
        return [("down", CH * (b + 1) - 1)]
    return {"aqk": [("asim", prev)], "av": [("aav", prev)], "aexp": [("aT", prev)], "ascale": [("asT", prev), ("amax", prev)],
            "ass": [("ascale", prev)], "aT": [("aav", prev)], "aav": [("y", prev)], "amax": [("aexp", prev)],
            "bqk": [("bs", prev, NT - 1)], "bs": [("bpT", prev, NT - 1)], "bvl": [("bo", prev, 1)],
            "bv": [("bvl", prev)], "bpT": [("bo", prev, 1)], "bexp": [("byx", prev), ("bsp", b, s[-1], 3)], "bo": [("by", prev)],
            "route": [("act", prev)], "rsum": [("actk", prev)], "actk": [("sbc", prev)]}.get(kind, [])


def plan():
    last = CH * 2 * NB
    threads = [thread("F", n, F_STEPS, CH * n - F_AHEAD) for n in range(2 * NB)]
    threads += [[CH * (n + 1) + 3, [(0, ("yT", n))], 0] for n in range(2 * NB - 1)]
    threads += [thread("B", b, B_STEPS, CH + 3 + B_EVERY * b) for b in range(NB)]
    threads += [thread("A", b, A_STEPS, A_STARTS[b]) for b in range(NB)]
    pieces = [("wp", j) for j in range(3 * CH // WCH)]
    steps, done, order = [], set(), {}
    free_after = []
    debt = [0.0, 0.0]

    def ready(s):
        if not all(v in done or v[1] == -1 for v in needs(s)):
            return False
        if s[0] == "xn" and order[s[1:]] >= 2:
            two_before = [v for v, i in order.items() if i == order[s[1:]] - 2][0]
            if ("xT",) + two_before not in done:
                return False
        if s[0] == "stats" and len(order) >= 2:
            two_before = [v for v, i in order.items() if i == len(order) - 2][0]
            if ("xn",) + two_before not in done:
                return False
        n = 0 if s[0] == "bo" and s[2] else TURNS.get(s[0], 0)
        return all(len(free_after) + i < 3 or free_after[len(free_after) + i - 3] in done for i in range(n))

    def add(s):
        steps.append(s)
        done.add(s)
        if s[0] == "stats":
            order[s[1:]] = len(order)
        if s[0] in TURNS and not (s[0] == "bo" and s[2]):
            by = s
            if s[0] == "xT" and s[1] != "A":
                by = ("xl",) + s[1:]
            if s[0] in FREED_BY:
                by = (FREED_BY[s[0]],) + (s[1:2] if s[0] == "bo" else s[1:])
            free_after.extend([by] * TURNS[s[0]])

    k = A_STARTS[0] - 1
    while k < last - 1:
        if k + 1 < 0 or (k + 1) % CH or ("sbc", (k + 1) // CH) in done:
            k += 1
        else:
            for th in threads:
                th[0] -= th[0] <= k
        if k >= 0 and ("um", k) not in done:
            if k >= 2:
                add(("gu", k))
            add(("um", k))
            if k >= LAG:
                add(("down", k - LAG))
            if k:
                add(("hl", k - 1))
        if pieces and (k >= 0 or k >= A_STARTS[0] + 5 and len(pieces) > 3 * CH // WCH - NSTAGE):
            add(pieces.pop(0))
        pe = 1.9
        act, dve = debt[0] + 1.0, debt[1] + 1.2
        for th in threads:
            while th[1] and th[0] + th[1][0][0] <= k:
                s = th[1][0][1]
                cost = COST.get(s[0], (0, 0, 0))
                late = k >= 0 and th[2] < SHIFTS and (act + cost[1] > pe + cost[0] + DEBT + (cost[1] > 2) * 3 or dve + cost[2] > pe + cost[0] + DEBT)
                if not ready(s) or late:
                    th[0] += 1
                    th[2] += 1
                    break
                th[1].pop(0)
                add(s)
                if s in GU_AFTER:
                    add(("gu", GU_AFTER[s]))
                pe, act, dve = pe + cost[0], act + cost[1], dve + cost[2]
        debt = [max(0.0, act - pe), max(0.0, dve - pe)]
    assert not any(th[1] for th in threads)
    for s in [("hl", last - 1), *[("down", k) for k in range(last - LAG, last)], ("yT", 2 * NB - 1)]:
        add(s)
    return steps, order


def build(nc, x_d, small_d, gate_d, up_d, down_d, w2_d, cols_d, rows_d, out_d):
    steps, norm_no = plan()
    turn_of = {}
    turns = 0
    for s in steps:
        if s[0] in TURNS and (s[0] != "bo" or s[2] == 0):
            turn_of[s] = turns
            turns += TURNS[s[0]]
    xT_turn = {norm_no[s[1:]]: turn_of[s] for s in steps if s[0] == "xT"}
    split_no = {s[1:]: i for i, s in enumerate(s for s in steps if s[0] == "xT" and s[1] != "A")}
    wrote = {("A", b): None for b in range(NB)}
    wrote |= {("F", b): ("y", b) for b in range(NB)} | {("B", b): ("yT", b) for b in range(NB)}
    wrote |= {("F", NB + b): ("by", b) for b in range(NB)}

    with ExitStack() as ctx:
        base = (nc.sbuf_base + 63) // 64 * 64
        cursor = [base]

        def sb(name, shape, dt=F32):
            size = 1
            for n in shape[1:]:
                size *= n
            size = (size * (2 if dt == BF16 else 4) + 31) // 32 * 32
            t = nc.alloc_sbuf_tensor_at(name, shape, dt, offset=cursor[0])
            cursor[0] += size
            return t

        X = sb("X", [P, NB * NT, D])
        WGh, WGl = (sb(n, [P, CH, P], F32R) for n in ("WGh", "WGl"))
        WUh, WUl = (sb(n, [P, CH, P], F32R) for n in ("WUh", "WUl"))
        WDh, WDl = (sb(n, [P, CH, P], F32R) for n in ("WDh", "WDl"))
        raw = sb("raw", [P, C_ALL])
        SWh, SWl = (sb(n, [P, C_ALL - C_BQKV], F32R) for n in ("SWh", "SWl"))
        ident = sb("ident", [P, P])
        w2 = sb("w2", [AH, KMAX + 2])
        cols = sb("cols", [P, 6])
        rows = sb("rows", [P, 272])
        bq = sb("bq", [P, 1])
        etemp = sb("etemp", [P, 1])
        ones = sb("ones", [P, P])
        hmask = sb("hmask", [P, P])
        nhalf = sb("nhalf", [P, NT])
        xhS, xlS = (sb(n, [P, T], F32R) for n in ("xhS", "xlS"))
        xhF = [sb(f"xhF{i}", [P, T], F32R) for i in range(2)]
        xlF = [sb(f"xlF{i}", [P, T], F32R) for i in range(2)]
        xns = [sb(f"xn{i}", [P, NT, D]) for i in range(2)]
        bst = sb("bst", [P, NT, 6])
        mvs = [sb(f"mv{i}", [P, NT, 2]) for i in range(2)]
        rstds = [sb(f"rstd{i}", [P, NT]) for i in range(2)]
        rts = [sb(f"rt{i}", [P, NT]) for i in range(2)]
        pe_ = sb("pe_", [P, NT, E])
        pr = sb("pr", [P, NT, E])
        p4 = sb("p4", [P, 6, NT])
        gt = sb("gt", [P, NT, E, E], BF16)
        ge = sb("ge", [P, NT, E, E], BF16)
        tri = sb("tri", [P, E, E], BF16)
        rk = sb("rk", [P, NT, E])
        al_ = sb("al_", [P, NT, KMAX])
        av_ = sb("av_", [P, NT, KMAX])
        kidx = sb("kidx", [P, NT, KMAX])
        sx = sb("sx", [P, NT, E, P // E])
        xa, hq = (sb(n, [AH, T]) for n in ("xa", "hq"))
        YT = sb("YT", [P, T])
        sbc = [sb(f"sbc{i}", [P, T]) for i in range(2)]
        sl = [sb(f"sl{i}", [P, T]) for i in range(2)]
        t2 = [sb(f"t2{i}", [P, T]) for i in range(3)]
        ah = [sb(f"ah{i}", [P, T], F32R) for i in range(2)]
        alo = [sb(f"alo{i}", [P, T], F32R) for i in range(2)]
        xaT = sb("xaT", [P, T])
        qk = sb("qk", [P, NT, 2, P])
        sq = sb("sq", [P, NT, 2, P])
        vT = sb("vT", [P, T])
        oA = sb("oA", [P, T])
        ss, rs = (sb(n, [P, 2]) for n in ("ss", "rs"))
        simT, sim, attn, attnT = (sb(n, [P, P]) for n in ("simT", "sim", "attn", "attnT"))
        qn, amx, ars, ari = (sb(n, [P, 1]) for n in ("qn", "amx", "ars", "ari"))
        mark = cursor[0]
        stage = [sb(f"stage{i}", [P, WCOLS]) for i in range(NSTAGE)]
        end = cursor[0]
        cursor[0] = mark
        qF, kF = (sb(n, [P, T]) for n in ("qF", "kF"))
        qh, ql, kh, kl = (sb(n, [P, T], F32R) for n in ("qh", "ql", "kh", "kl"))
        vF = sb("vF", [P, NT, D])
        vh, vl = (sb(n, [P, NT, D], F32R) for n in ("vh", "vl"))
        Sb = sb("Sb", [P, NT, T])
        mk = [sb(f"mk{i}", [P, T], BF16) for i in range(4)]
        PTh, PTl = (sb(n, [P, NT, T], F32R) for n in ("PTh", "PTl"))
        oTh, oTl = (sb(n, [P, T], F32R) for n in ("oTh", "oTl"))
        bmx = sb("bmx", [P, NT])
        brs = sb("brs", [P, NT])
        bri = sb("bri", [P, NT])
        bt = sb("bt", [P, NT, D])
        cursor[0] = max(end, cursor[0])
        assert cursor[0] <= nc.sbuf_usable_end, cursor[0] - nc.sbuf_usable_end

        bank = [ctx.enter_context(nc.psum_tensor(f"bank{i}", [P, 512], F32)) for i in range(8)]
        OACC = bank[7]

        def sem(name):
            return ctx.enter_context(nc.semaphore(name))

        x_loaded = [sem(f"x_loaded{b}") for b in range(NB)]
        small_loaded = sem("small_loaded")
        rows_loaded = sem("rows_loaded")
        stage_loaded = [sem(f"stage_loaded{i}") for i in range(NSTAGE)]
        consts_ready = sem("consts_ready")
        pool_did = sem("pool_did")
        dve_did = sem("dve_did")
        etemp_ready = sem("etemp_ready")
        bq_ready = sem("bq_ready")
        wn_ready = sem("wn_ready")
        swh_ready, swl_ready = sem("swh_ready"), sem("swl_ready")
        wh_ready, wl_dve, wl_pool = sem("wh_ready"), sem("wl_dve"), sem("wl_pool")
        stats_ready, rstd_ready, xn_ready, xh_ready = (sem(n) for n in ("stats_ready", "rstd_ready", "xn_ready", "xh_ready"))
        m_full = [sem(f"m_full{i}") for i in range(3)]
        m_free = [sem(f"m_free{i}") for i in range(3)]
        sums_ready, norms_ready, simT_ready, simx_ready, aexp_done, ari_ready = (
            sem(n) for n in ("sums_ready", "norms_ready", "simT_ready", "simx_ready", "aexp_done", "ari_ready"))
        exp8_ready, factor_ready, inner_ready, th_ready, g_ready, sx_ready = (
            sem(n) for n in ("exp8_ready", "factor_ready", "inner_ready", "th_ready", "g_ready", "sx_ready"))
        pr_ready = sem("pr_ready")
        pe_sub = sem("pe_sub")
        g_full, silu_done, u_full, t2_done, a_done = (sem(n) for n in ("g_full", "silu_done", "u_full", "t2_done", "a_done"))
        ahi_done, alo_done, down_done, y_free = (sem(n) for n in ("ahi_done", "alo_done", "down_done", "y_free"))
        qf_ready, qh_ready, qkl_ready, v_ready = (sem(n) for n in ("qf_ready", "qh_ready", "qkl_ready", "v_ready"))
        sp_ready, bexp_done = sem("sp_ready"), sem("bexp_done")
        pth_ready, oth_ready = sem("pth_ready"), sem("oth_ready")
        mk_ready = sem("mk_ready")
        stored = sem("stored")

        def m_bank(t):
            return bank[4 + t % 3]

        def wait_full(eng, t):
            eng.wait_ge(m_full[t % 3], t // 3 + 1)

        def wait_free(eng, t):
            eng.wait_ge(m_free[t % 3], t // 3 + 1)

        def n_free(t):
            return m_free[t % 3]

        def piece_of(j):
            hi, lo = ((WGh, WGl), (WUh, WUl), (WDh, WDl))[j % 3]
            at = slice(j // 3 * WCOLS, j // 3 * WCOLS + WCOLS)
            return (w[:, :, :].rearrange("p c n -> p (c n)")[:, at] for w in (hi, lo))

        block = ctx.enter_context(nc.Block())

        @block.sync
        def _(sp):
            xv = x_d.rearrange("b (i p) c -> p b i c", p=P)
            sp.dma_start(X[:, 0:NT, :], xv[:, 0]).then_inc(x_loaded[0], 16)
            sp.dma_start(raw[:, :], small_d).then_inc(small_loaded, 16)
            sp.dma_start(cols[:, :], cols_d).then_inc(small_loaded, 16)
            sp.dma_start(X[:, NT:2 * NT, :], xv[:, 1]).then_inc(x_loaded[1], 16)
            sp.dma_start(rows[:, :], rows_d.partition_broadcast(P)).then_inc(rows_loaded, 16)
            sp.dma_start(w2[:, 0:KMAX], w2_d).then_inc(small_loaded, 16)
            for s in steps:
                if s[0] == "wp":
                    j = s[1]
                    if j >= NSTAGE:
                        i = j - NSTAGE
                        sp.wait_ge(wl_pool if i % 3 == 2 else wl_dve, i // 3 + 1 if i % 3 == 2 else i // 3 * 2 + i % 3 + 1)
                    at = j // 3 * WCOLS
                    sp.dma_start(stage[j % NSTAGE][:, :], (gate_d, up_d, down_d)[j % 3][:, at:at + WCOLS])\
                      .then_inc(stage_loaded[j % NSTAGE], 16)
                    if NSTAGE <= j < NSTAGE + NB - 2:
                        b = j - NSTAGE + 2
                        sp.dma_start(X[:, NT * b:NT * b + NT, :], xv[:, b]).then_inc(x_loaded[b], 16)
            for b in range(NB):
                wait_free(sp, turn_of["yT", NB + b])
                sp.dma_start(out_d.rearrange("b (i p) c -> p b i c", p=P)[:, b], X[:, NT * b:NT * b + NT, :])\
                  .then_inc(stored, 16)
            sp.wait_ge(stored, 16 * NB)

        @block.gpsimd
        def _(pool):
            did = [0]

            def chain(ins):
                did[0] += 1
                ins.then_inc(pool_did, 1)
                pool.wait_ge(pool_did, did[0])

            def head_mask():
                for e in range(H):
                    own = hmask[:, e * DH:e * DH + DH]
                    chain(pool.memset(own, 0.0))
                    chain(pool.affine_select(out=own, in_=own, compare_op=ALU.is_ge, fill=NEG, base=-e * DH,
                                             pattern=[[0, DH]], channel_multiplier=1))
                    r = pool.affine_select(out=own, in_=own, compare_op=ALU.is_ge, fill=NEG, base=e * DH + DH - 1,
                                           pattern=[[0, DH]], channel_multiplier=-1)
                r.then_inc(consts_ready, 1)

            chain(pool.memset(ident[:, :], 0.0))
            chain(pool.affine_select(out=ident[:, :], in_=ident[:, :], compare_op=ALU.not_equal, fill=1.0,
                                     base=0, pattern=[[-1, P]], channel_multiplier=1))
            pool.memset(ones[:, :], 1.0)
            pool.memset(nhalf[:, :], -0.5).then_inc(consts_ready, 1)

            for s in steps:
                kind = s[0]
                if kind == "stats":
                    _, what, b = s
                    seq = norm_no[what, b]
                    if seq == 0:
                        pool.wait_ge(consts_ready, 1)
                    pool.wait_ge(stats_ready, seq + 1)
                    mv, rt, rstd = mvs[seq % 2], rts[seq % 2], rstds[seq % 2]
                    if seq >= 2:
                        pool.wait_ge(xn_ready, seq - 1)
                    by, more = (1.0 + RMS_EPS, RMS_EPS * LN_EPS) if what == "A" else (1.0, LN_EPS)
                    chain(pool.tensor_scalar(rt[:, :], mv[:, :, 1], by, more, ALU.mult, ALU.add))
                    pool.tensor_tensor(rstd[:, :], rt[:, :], nhalf[:, :], ALU.pow).then_inc(rstd_ready, 1)
                    if seq == 0:
                        head_mask()
                if kind == "ass":
                    b = s[1]
                    pool.wait_ge(sums_ready, b + 1)
                    if b:
                        wait_free(pool, turn_of["asT", b - 1])
                    pool.tensor_tensor(rs[:, :], ss[:, :], nhalf[:, 0:2], ALU.pow).then_inc(norms_ready, 1)
                if kind == "wp" and s[1] % 3 == 2:
                    j = s[1]
                    pool.wait_ge(wh_ready, j + 1)
                    hi, lo = piece_of(j)
                    pool.tensor_tensor(lo, stage[j % NSTAGE][:, :], hi.bitcast(F32), ALU.subtract).then_inc(wl_pool, 1)
                if kind == "inner" and s[2] == 0:
                    wait_free(pool, turn_of["route", s[1]] + 1)
                    pool.tensor_scalar(hq[:, :], hq[:, :], 0.044715, 1.0, ALU.mult, ALU.add).then_inc(factor_ready, 1)
                if kind == "inner" and s[2] == 1:
                    pool.wait_ge(factor_ready, s[1] + 1)
                    pool.tensor_tensor(hq[:, :], hq[:, :], xa[:, :], ALU.mult).then_inc(inner_ready, 1)
                if kind == "um":
                    k = s[1]
                    pool.wait_ge(t2_done, k + 1)
                    pool.wait_ge(silu_done, k + 1)
                    pool.tensor_tensor(t2[k % 3][:, :], t2[k % 3][:, :], sl[k % 2][:, :], ALU.mult).then_inc(a_done, 1)

        @block.scalar
        def _(act):
            act.wait_ge(small_loaded, 48)
            act.activation(etemp[:, :], cols[:, 5:6], ACT.Exp).then_inc(etemp_ready, 1)
            act.activation(SWh[:, :], raw[:, C_BQKV:C_ALL], ACT.Copy).then_inc(swh_ready, 1)
            act.activation(bq[:, :], cols[:, 1:2], ACT.Copy, scale=B_SCALE).then_inc(bq_ready, 1)

            for s in steps:
                kind = s[0]
                if kind == "xT":
                    _, what, b = s
                    t = turn_of[s]
                    wait_full(act, t)
                    if what == "A":
                        if b:
                            wait_full(act, turn_of["av", b - 1])
                        act.activation(xaT[:, :], m_bank(t)[:, :], ACT.Copy).then_inc(n_free(t), 1)
                        continue
                    if what == "F" and b >= 2:
                        act.wait_ge(u_full, CH * (b - 1))
                    if what == "B" and b:
                        wait_full(act, turn_of["bv", b - 1])
                    dst = xhF[b % 2] if what == "F" else xhS
                    act.activation(dst[:, :], m_bank(t)[:, :], ACT.Copy).then_inc(xh_ready, 1)
                if kind == "aqk":
                    _, b, j = s
                    t = turn_of[s]
                    if b:
                        wait_full(act, turn_of["asim", b - 1])
                    wait_full(act, t)
                    tiles = m_bank(t)[:, :].rearrange("p (i r c) -> p i r c", i=2, r=2)
                    act.activation(sq[:, 2 * j:2 * j + 2, :, :], tiles, ACT.Square)
                    act.activation(qk[:, 2 * j:2 * j + 2, :, :], tiles, ACT.Copy).then_inc(n_free(t), 1)
                if kind == "av":
                    b = s[1]
                    t = turn_of[s]
                    wait_full(act, t)
                    if b:
                        wait_full(act, turn_of["aav", b - 1])
                    act.activation(vT[:, :], m_bank(t)[:, :], ACT.Copy).then_inc(n_free(t), 1)
                if kind == "aexp":
                    b = s[1]
                    act.wait_ge(simx_ready, b + 1)
                    if b:
                        wait_full(act, turn_of["aT", b - 1])
                    act.activation(attn[:, :], sim[:, :], ACT.Exp, bias=amx[:, 0:1], accum_out=ars[:, 0:1])\
                       .then_inc(aexp_done, 1)
                if kind == "aT":
                    b = s[1]
                    t = turn_of[s]
                    wait_full(act, t)
                    act.activation(attnT[:, :], m_bank(t)[:, 0:P], ACT.Copy).then_inc(n_free(t), 1)
                if kind == "aav":
                    b = s[1]
                    t = turn_of[s]
                    wait_full(act, t)
                    if b:
                        wait_full(act, turn_of["y", b - 1])
                    act.wait_ge(ari_ready, b + 1)
                    act.activation(oA[:, :], m_bank(t)[:, :], ACT.Copy, scale=ari[:, 0:1]).then_inc(n_free(t), 1)
                if kind == "wp":
                    j = s[1]
                    act.wait_ge(stage_loaded[j % NSTAGE], 16 * (j // NSTAGE + 1))
                    hi, _lo = piece_of(j)
                    act.activation(hi, stage[j % NSTAGE][:, :], ACT.Copy).then_inc(wh_ready, 1)
                if kind == "rexp":
                    act.wait_ge(pe_sub, s[1] + 1)
                    act.activation(pe_[:, :, :], pe_[:, :, :], ACT.Exp).then_inc(exp8_ready, 1)
                if kind == "route":
                    n = s[1]
                    t = turn_of[s]
                    wait_full(act, t + 1)
                    if n:
                        wait_full(act, turn_of["act", n - 1])
                    act.activation(xa[:, :], m_bank(t + 1)[0:AH, :], ACT.Identity, bias=cols[0:AH, 4:5])
                    act.activation(hq[:, :], m_bank(t + 1)[0:AH, :], ACT.Square, bias=cols[0:AH, 4:5])\
                       .then_inc(n_free(t + 1), 1)
                if kind == "tanh":
                    n = s[1]
                    act.wait_ge(inner_ready, n + 1)
                    act.activation(hq[:, :], hq[:, :], ACT.Tanh, scale=0.7978845608028654).then_inc(th_ready, 1)
                if kind == "sbc":
                    n = s[1]
                    t = turn_of[s]
                    wait_full(act, t)
                    if n >= 2:
                        act.wait_ge(t2_done, CH * (n - 1))
                    act.activation(sbc[n % 2][:, :], m_bank(t)[:, :], ACT.Copy).then_inc(n_free(t), 1)
                if kind == "gu":
                    k = s[1]
                    act.wait_ge(g_full, k + 1)
                    if k >= 2:
                        act.wait_ge(a_done, k - 1)
                    act.activation(sl[k % 2][:, :], bank[k % 2][:, :], ACT.Silu).then_inc(silu_done, 1)
                if kind == "hl":
                    k = s[1]
                    act.wait_ge(a_done, k + 1)
                    if k >= 2:
                        act.wait_ge(down_done, k - 1)
                    act.activation(ah[k % 2][:, :], t2[k % 3][:, :], ACT.Copy).then_inc(ahi_done, 1)
                if kind == "down" and s[1] % CH == CH - 1:
                    n = s[1] // CH
                    act.wait_ge(down_done, CH * (n + 1))
                    if n:
                        wait_full(act, turn_of["yT", n - 1])
                    act.activation(YT[:, :], OACC[:, :], ACT.Copy).then_inc(y_free, 1)
                if kind == "bqk":
                    _, b, j = s
                    t = turn_of[s]
                    if b == 0 and j == 0:
                        act.wait_ge(bq_ready, 1)
                    if b:
                        wait_full(act, turn_of["bs", b - 1, NT - 1])
                        act.wait_ge(qkl_ready, 2 * b)
                    wait_full(act, t)
                    full, hi = ((qF, qh), (kF, kh))[j]
                    if j == 0:
                        act.activation(full[:, :], m_bank(t)[:, :], ACT.Identity, bias=bq[:, 0:1], scale=B_SCALE)\
                           .then_inc(qf_ready, 1)
                    else:
                        act.activation(full[:, :], m_bank(t)[:, :], ACT.Identity, bias=cols[:, 2:3]).then_inc(qf_ready, 1)
                    act.wait_ge(qf_ready, 2 * b + j + 1)
                    act.activation(hi[:, :], full[:, :], ACT.Copy).then_inc(n_free(t), 1)
                if kind == "bs":
                    _, b, i = s
                    t = turn_of[s]
                    wait_full(act, t)
                    if b:
                        wait_full(act, turn_of["bpT", b - 1, NT - 1])
                    act.activation(Sb[:, i, :], m_bank(t)[:, :], ACT.Copy).then_inc(n_free(t), 1)
                if kind == "bexp":
                    _, b, i = s
                    act.wait_ge(sp_ready, NT * b + i + 1)
                    act.activation(Sb[:, i, :], Sb[:, i, :], ACT.Exp, bias=bmx[:, i:i + 1],
                                   accum_out=brs[:, i:i + 1]).then_inc(bexp_done, 1)
                if kind == "bpT":
                    _, b, j = s
                    t = turn_of[s]
                    wait_full(act, t)
                    if b:
                        wait_full(act, turn_of["bo", b - 1, 0])
                    act.activation(PTh[:, j, :], m_bank(t)[:, :], ACT.Copy).then_inc(pth_ready, 1)
                if kind == "bo" and s[2] == 1:
                    b = s[1]
                    t = turn_of["bo", b, 0]
                    wait_full(act, t)
                    if b:
                        wait_full(act, turn_of["by", b - 1])
                    act.activation(oTh[:, :], m_bank(t)[:, :], ACT.Copy).then_inc(oth_ready, 1)

        @block.vector
        def _(dve):
            did = [0]

            def chain(ins):
                did[0] += 1
                ins.then_inc(dve_did, 1)
                dve.wait_ge(dve_did, did[0])

            for e in range(E):
                if e:
                    dve.memset(tri[:, e, 0:e], 1.0)
                dve.memset(tri[:, e, e:E], 0.0)
            for j in range(KMAX):
                r = dve.memset(kidx[:, :, j:j + 1], float(j + 1))
            chain(r)

            for s in steps:
                kind = s[0]
                if kind == "stats":
                    _, what, b = s
                    q = b % NB
                    seq = norm_no[what, b]
                    src = wrote[what, b]
                    if src is None:
                        dve.wait_ge(x_loaded[q], 16)
                    else:
                        wait_free(dve, turn_of[src])
                    mv = mvs[seq % 2]
                    if seq:
                        dve.wait_ge(stats_ready, seq)
                    for i in range(NT):
                        r = dve.bn_stats(bst[:, i, :], X[:, NT * q + i, :])
                    chain(r)
                    for i in range(NT):
                        r = dve.bn_aggr(mv[:, i, :], bst[:, i, :])
                    r.then_inc(stats_ready, 1)
                if kind == "xn":
                    _, what, b = s
                    q = b % NB
                    seq = norm_no[what, b]
                    mv, rstd, xn = mvs[seq % 2], rstds[seq % 2], xns[seq % 2]
                    if seq >= 2:
                        wait_full(dve, xT_turn[seq - 2])
                    dve.wait_ge(rstd_ready, seq + 1)
                    for i in range(NT):
                        r = dve.tensor_scalar(xn[:, i, :], X[:, NT * q + i, :], mv[:, i, 0:1], rstd[:, i:i + 1],
                                              ALU.subtract, ALU.mult)
                    r.then_inc(xn_ready, 1)
                    if seq == 0:
                        dve.wait_ge(small_loaded, 48)
                        dve.tensor_scalar(raw[:, 0:384], raw[:, 0:384], cols[:, 0:1], None, ALU.mult).then_inc(wn_ready, 1)
                        dve.wait_ge(wn_ready, 1)
                        dve.wait_ge(swh_ready, 1)
                        dve.tensor_tensor(SWl[:, :], raw[:, C_BQKV:C_ALL], SWh[:, :].bitcast(F32), ALU.subtract)\
                           .then_inc(swl_ready, 1)
                if kind == "xl":
                    _, what, b = s
                    t = turn_of["xT", what, b]
                    dst, hi = (xlF[b % 2], xhF[b % 2]) if what == "F" else (xlS, xhS)
                    dve.wait_ge(xh_ready, split_no[what, b] + 1)
                    if what == "B" and b:
                        wait_full(dve, turn_of["bv", b - 1])
                    dve.tensor_tensor(dst[:, :], m_bank(t)[:, :], hi[:, :].bitcast(F32), ALU.subtract).then_inc(n_free(t), 1)
                if kind == "wp" and s[1] % 3 != 2:
                    j = s[1]
                    dve.wait_ge(wh_ready, j + 1)
                    hi, lo = piece_of(j)
                    dve.tensor_tensor(lo, stage[j % NSTAGE][:, :], hi.bitcast(F32), ALU.subtract).then_inc(wl_dve, 1)
                if kind == "ass":
                    b = s[1]
                    t = turn_of["asim", b]
                    wait_full(dve, t)
                    if b:
                        dve.wait_ge(norms_ready, b)
                    dve.tensor_scalar(ss[:, :], m_bank(t)[:, P:P + 2], 1e-24, None, ALU.max).then_inc(sums_ready, 1)
                if kind == "ascale":
                    b = s[1]
                    t = turn_of["asim", b]
                    dve.wait_ge(norms_ready, b + 1)
                    if b == 0:
                        dve.wait_ge(etemp_ready, 1)
                    dve.tensor_tensor(qn[:, :], rs[:, 1:2], etemp[:, 0:1], ALU.mult)
                    dve.tensor_scalar(simT[:, :], m_bank(t)[:, 0:P], rs[:, 0:1], None, ALU.mult).then_inc(n_free(t), 1)
                if kind == "amax":
                    b = s[1]
                    t = turn_of["asT", b]
                    if b == 0:
                        dve.wait_ge(consts_ready, 2)
                    else:
                        dve.wait_ge(aexp_done, b)
                    wait_full(dve, t)
                    dve.scalar_tensor_tensor(sim[:, :], m_bank(t)[:, 0:P], qn[:, 0:1], hmask[:, :], ALU.mult, ALU.add)\
                       .then_inc(n_free(t), 1)
                    wait_free(dve, t)
                    dve.tensor_reduce(amx[:, 0:1], sim[:, :], AX_X, ALU.max, negate=True).then_inc(simx_ready, 1)
                if kind == "aT":
                    b = s[1]
                    dve.wait_ge(aexp_done, b + 1)
                    if b:
                        wait_free(dve, turn_of["aav", b - 1])
                    dve.reciprocal(ari[:, :], ars[:, :]).then_inc(ari_ready, 1)
                if kind in ("y", "yT"):
                    t = turn_of[s]
                    q = s[1] % NB
                    wait_full(dve, t)
                    xs = X[:, NT * q:NT * q + NT, :].rearrange("p i d -> p (i d)")
                    dve.tensor_tensor(xs, m_bank(t)[:, :], xs, ALU.add).then_inc(n_free(t), 1)
                if kind == "route":
                    n = s[1]
                    t = turn_of[s]
                    wait_full(dve, t)
                    lg = m_bank(t)[:, 0:NT * E].rearrange("p (i e) -> p i e", e=E)
                    chain(dve.tensor_reduce(p4[:, 0], lg, AX_X, ALU.max))
                    dve.tensor_tensor(pe_[:, :, :], lg, p4[:, 0].unsqueeze(2).to_broadcast([P, NT, E]),
                                      ALU.subtract).then_inc(pe_sub, 1)
                    dve.wait_ge(pe_sub, n + 1)
                    dve.tensor_copy(p4[:, 5], p4[:, 0]).then_inc(n_free(t), 1)
                if kind == "rsum":
                    n = s[1]
                    dve.wait_ge(exp8_ready, n + 1)
                    chain(dve.tensor_reduce(p4[:, 1], pe_[:, :, :], AX_X, ALU.add))
                    chain(dve.reciprocal(p4[:, 2], p4[:, 1]))
                    chain(dve.tensor_tensor(pr[:, :, :], pe_[:, :, :], p4[:, 2].unsqueeze(2).to_broadcast([P, NT, E]), ALU.mult))
                    other = pr[:, :, :].unsqueeze(2).to_broadcast([P, NT, E, E])
                    own = pr[:, :, :].unsqueeze(3).to_broadcast([P, NT, E, E])
                    dve.tensor_tensor(gt[:, :, :, :], other, own, ALU.is_gt)
                    dve.tensor_tensor(ge[:, :, :, :], other, own, ALU.is_ge).then_inc(pr_ready, 1)
                if kind == "rrank":
                    n = s[1]
                    dve.wait_ge(pr_ready, n + 1)
                    chain(dve.tensor_tensor(ge[:, :, :, :], ge[:, :, :, :],
                                            tri[:, :, :].unsqueeze(1).to_broadcast([P, NT, E, E]), ALU.mult))
                    chain(dve.tensor_tensor(gt[:, :, :, :], gt[:, :, :, :], ge[:, :, :, :], ALU.max))
                    chain(dve.tensor_reduce(rk[:, :, :], gt[:, :, :, :], AX_X, ALU.add))
                if kind == "gelu":
                    n = s[1]
                    dve.wait_ge(th_ready, n + 1)
                    dve.scalar_tensor_tensor(hq[:, :], hq[:, :], 1.0, xa[:, :], ALU.add, ALU.mult).then_inc(g_ready, 1)
                if kind == "actk":
                    n = s[1]
                    t = turn_of["act", n]
                    if n == 0:
                        dve.wait_ge(rows_loaded, 16)
                    wait_full(dve, t)
                    lg = m_bank(t)[:, 0:NT * 8].rearrange("p (i e) -> p i e", e=8)[:, :, 0:KMAX]
                    dve.scalar_tensor_tensor(al_[:, :, :], lg, 0.5,
                                             rows[:, 256:262].unsqueeze(1).to_broadcast([P, NT, KMAX]),
                                             ALU.mult, ALU.add).then_inc(n_free(t), 1)
                    wait_free(dve, t)
                    chain(dve.tensor_scalar(al_[:, :, :], al_[:, :, :], 30.0, -30.0, ALU.min, ALU.max))
                    chain(dve.tensor_reduce(p4[:, 3], al_[:, :, :], AX_X, ALU.max))
                    chain(dve.tensor_tensor(av_[:, :, :], al_[:, :, :], p4[:, 3].unsqueeze(2).to_broadcast([P, NT, KMAX]), ALU.is_ge))
                    chain(dve.scalar_tensor_tensor(av_[:, :, :], av_[:, :, :], -16.0, kidx[:, :, :], ALU.mult, ALU.add))
                    chain(dve.tensor_reduce(p4[:, 4], av_[:, :, :], AX_X, ALU.min))
                    chain(dve.scalar_tensor_tensor(rk[:, :, :], rk[:, :, :], -16.0,
                                                   p4[:, 4].unsqueeze(2).to_broadcast([P, NT, E]), ALU.add, ALU.is_lt))
                    if n:
                        wait_full(dve, turn_of["sbc", n - 1])
                    dve.tensor_tensor(sx[:, :, :, :], rk[:, :, :].unsqueeze(3).to_broadcast([P, NT, E, P // E]),
                                      pr[:, :, :].unsqueeze(3).to_broadcast([P, NT, E, P // E]), ALU.mult).then_inc(sx_ready, 1)
                if kind == "um":
                    k = s[1]
                    if k % CH == 0:
                        wait_free(dve, turn_of["sbc", k // CH])
                    dve.wait_ge(u_full, k + 1)
                    if k >= 3:
                        dve.wait_ge(alo_done, k - 2)
                    dve.tensor_tensor(t2[k % 3][:, :], bank[2 + k % 2][:, :], sbc[k // CH % 2][:, :],
                                      ALU.mult).then_inc(t2_done, 1)
                if kind == "hl":
                    k = s[1]
                    dve.wait_ge(ahi_done, k + 1)
                    if k >= 2:
                        dve.wait_ge(down_done, k - 1)
                    dve.tensor_tensor(alo[k % 2][:, :], t2[k % 3][:, :], ah[k % 2][:, :].bitcast(F32),
                                      ALU.subtract).then_inc(alo_done, 1)
                if kind == "bqkl":
                    _, b, j = s
                    wait_free(dve, turn_of["bqk", b, j])
                    full, hi, lo = ((qF, qh, ql), (kF, kh, kl))[j]
                    dve.tensor_tensor(lo[:, :], full[:, :], hi[:, :].bitcast(F32), ALU.subtract).then_inc(qkl_ready, 1)
                if kind == "bv":
                    b = s[1]
                    t = turn_of[s]
                    wait_full(dve, t)
                    dve.tensor_tensor(vF[:, :, :], m_bank(t)[:, :].rearrange("p (i d) -> p i d", d=D),
                                      rows[:, 0:P].unsqueeze(1).to_broadcast([P, NT, D]), ALU.add).then_inc(n_free(t), 1)
                if kind == "bvl":
                    b = s[1]
                    wait_free(dve, turn_of["bv", b])
                    if b:
                        wait_full(dve, turn_of["bo", b - 1, 0])
                    chain(dve.tensor_copy(vh[:, :, :], vF[:, :, :]))
                    dve.tensor_tensor(vl[:, :, :], vF[:, :, :], vh[:, :, :].bitcast(F32), ALU.subtract).then_inc(v_ready, 1)
                if kind == "bsp":
                    _, b, i, part = s
                    x_ = Sb[:, i, :]
                    step_no = 3 * (NT * b + i)
                    if part == 0:
                        wait_free(dve, turn_of["bs", b, i])
                        dve.tensor_scalar(mk[0][:, :], x_, X10 / 10, 2.0, ALU.is_ge, ALU.mult)
                        chain(dve.tensor_scalar(mk[1][:, :], x_, X25 / 10, 7.0, ALU.is_ge, ALU.mult))
                        dve.tensor_tensor(mk[0][:, :], mk[0][:, :], mk[1][:, :], ALU.add).then_inc(mk_ready, 1)
                    if part == 1:
                        dve.tensor_scalar(mk[2][:, :], x_, X85 / 10, 5.0, ALU.is_gt, ALU.mult)
                        chain(dve.tensor_scalar(mk[3][:, :], x_, X95 / 10, 5.0, ALU.is_gt, ALU.mult))
                        dve.tensor_tensor(mk[2][:, :], mk[2][:, :], mk[3][:, :], ALU.add).then_inc(mk_ready, 1)
                    if part == 2:
                        dve.wait_ge(mk_ready, step_no + 2)
                        chain(dve.tensor_tensor(mk[0][:, :], mk[0][:, :], mk[2][:, :], ALU.add))
                        dve.scalar_tensor_tensor(x_, mk[0][:, :], 1.0, x_, ALU.add, ALU.mult).then_inc(mk_ready, 1)
                    if part == 3:
                        dve.wait_ge(mk_ready, step_no + 3)
                        dve.tensor_reduce(bmx[:, i:i + 1], x_, AX_X, ALU.max, negate=True).then_inc(sp_ready, 1)
                if kind == "bpl":
                    _, b, j = s
                    t = turn_of["bpT", b, j]
                    dve.wait_ge(pth_ready, NT * b + j + 1)
                    if b:
                        wait_full(dve, turn_of["bo", b - 1, 0])
                    dve.tensor_tensor(PTl[:, j, :], m_bank(t)[:, :], PTh[:, j, :].bitcast(F32), ALU.subtract).then_inc(n_free(t), 1)
                    if j == 0:
                        dve.reciprocal(bri[:, :], brs[:, :])
                if kind == "bol":
                    b = s[1]
                    t = turn_of["bo", b, 0]
                    dve.wait_ge(oth_ready, b + 1)
                    dve.tensor_tensor(oTl[:, :], m_bank(t)[:, :], oTh[:, :].bitcast(F32), ALU.subtract).then_inc(n_free(t), 1)
                if kind == "byx":
                    b = s[1]
                    t = turn_of["by", b]
                    wait_full(dve, t)
                    for i in range(NT):
                        r = dve.scalar_tensor_tensor(bt[:, i, :], m_bank(t)[:, i * P:i * P + P], bri[:, i:i + 1],
                                                     rows[:, P:2 * P], ALU.mult, ALU.add)
                    chain(r)
                    xs = X[:, NT * b:NT * b + NT, :]
                    dve.tensor_tensor(xs, xs, bt[:, :, :], ALU.add).then_inc(n_free(t), 1)

        @block.tensor
        def _(pe):
            def turn(t):
                if t >= 3:
                    wait_free(pe, t - 3)
                return m_bank(t)

            def three(out, lh, ll, rh, rl, start=True, stop=True):
                pe.matmul(out, lh, rh, start=start, stop=False)
                pe.matmul(out, lh, rl, start=False, stop=False)
                return pe.matmul(out, ll, rh, start=False, stop=stop)

            def swide(c, n):
                return SWh[:, c - C_BQKV:c - C_BQKV + n], SWl[:, c - C_BQKV:c - C_BQKV + n]

            pe.wait_ge(consts_ready, 1)
            for s in steps:
                kind = s[0]
                if kind == "xT":
                    _, what, b = s
                    t = turn_of[s]
                    pe.wait_ge(xn_ready, norm_no[what, b] + 1)
                    xn = xns[norm_no[what, b] % 2]
                    m = turn(t)
                    for i in range(NT):
                        r = pe.transpose(m[:, i * P:i * P + P], xn[:, i, :], ident[:, :])
                    r.then_inc(m_full[t % 3], 1)
                if kind == "aqk":
                    _, b, j = s
                    t = turn_of[s]
                    if b == 0:
                        pe.wait_ge(wn_ready, 1)
                    wait_free(pe, turn_of["xT", "A", b])
                    m = turn(t)
                    for i in range(2):
                        r = pe.matmul(m[:, 256 * i:256 * i + 256], xaT[:, (2 * j + i) * P:(2 * j + i) * P + P],
                                      raw[:, C_QKV:C_QKV + 256], start=True, stop=True)
                    r.then_inc(m_full[t % 3], 1)
                if kind == "av":
                    b = s[1]
                    t = turn_of[s]
                    pe.matmul(turn(t)[:, :], raw[:, C_QKV + 256:C_QKV + 384], xaT[:, :], start=True, stop=True)\
                      .then_inc(m_full[t % 3], 1)
                if kind == "asim":
                    b = s[1]
                    t = turn_of[s]
                    m = turn(t)
                    wait_free(pe, turn_of["aqk", b, 0])
                    wait_free(pe, turn_of["aqk", b, 1])
                    for i in range(NT):
                        pe.matmul(m[:, 0:P], qk[:, i, 1, :], qk[:, i, 0, :], start=(i == 0), stop=(i == NT - 1))
                    for j in range(2):
                        for i in range(NT):
                            r = pe.matmul(m[:, P + j:P + j + 1], sq[:, i, 1 - j, :], ones[:, 0:1],
                                          start=(i == 0), stop=(i == NT - 1))
                    r.then_inc(m_full[t % 3], 1)
                if kind == "asT":
                    b = s[1]
                    t = turn_of[s]
                    wait_free(pe, turn_of["asim", b])
                    pe.transpose(turn(t)[:, 0:P], simT[:, :], ident[:, :]).then_inc(m_full[t % 3], 1)
                if kind == "aT":
                    b = s[1]
                    t = turn_of[s]
                    pe.wait_ge(aexp_done, b + 1)
                    pe.transpose(turn(t)[:, 0:P], attn[:, :], ident[:, :]).then_inc(m_full[t % 3], 1)
                if kind == "aav":
                    b = s[1]
                    t = turn_of[s]
                    wait_free(pe, turn_of["aT", b])
                    pe.matmul(turn(t)[:, :], attnT[:, :], vT[:, :], start=True, stop=True).then_inc(m_full[t % 3], 1)
                if kind == "y":
                    b = s[1]
                    t = turn_of[s]
                    wait_free(pe, turn_of["aav", b])
                    m = turn(t)
                    for i in range(NT):
                        a = slice(i * P, i * P + P)
                        r = pe.matmul(m[:, a], oA[:, a], raw[:, C_OUT:C_OUT + P], start=True, stop=True)
                    r.then_inc(m_full[t % 3], 1)
                if kind == "route":
                    n = s[1]
                    t = turn_of[s]
                    if n == 0:
                        pe.wait_ge(swl_ready, 1)
                    wait_free(pe, turn_of["xT", "F", n])
                    xh, xl = xhF[n % 2], xlF[n % 2]
                    m = turn(t)
                    wh, wl = swide(C_ROUTER, E)
                    for i in range(NT):
                        a = slice(i * P, i * P + P)
                        r = three(m[:, i * E:i * E + E], xh[:, a], xl[:, a], wh, wl)
                    r.then_inc(m_full[t % 3], 1)
                    m = turn(t + 1)
                    wh, wl = swide(C_ACTOR, P)
                    three(m[:, :], wh, wl, xh[:, :], xl[:, :]).then_inc(m_full[(t + 1) % 3], 1)
                if kind == "act":
                    n = s[1]
                    t = turn_of[s]
                    pe.wait_ge(g_ready, n + 1)
                    m = turn(t)
                    for i in range(NT):
                        r = pe.matmul(m[:, 8 * i:8 * i + KMAX], hq[:, i * P:i * P + P], w2[:, 0:KMAX], start=True, stop=True)
                    r.then_inc(m_full[t % 3], 1)
                if kind == "sbc":
                    n = s[1]
                    t = turn_of[s]
                    pe.wait_ge(sx_ready, n + 1)
                    m = turn(t)
                    for i in range(NT):
                        r = pe.transpose(m[:, i * P:i * P + P], sx[:, i, :, :].rearrange("p e r -> p (e r)"), ident[:, :])
                    r.then_inc(m_full[t % 3], 1)
                if kind == "gu":
                    k = s[1]
                    n, c = k // CH, k % CH
                    if k < CH and c % WCH == 0:
                        pe.wait_ge(wl_dve, 2 * (c // WCH) + 2)
                    if c == 0:
                        wait_free(pe, turn_of["xT", "F", n])
                    xh, xl = xhF[n % 2][:, :], xlF[n % 2][:, :]
                    if k >= 2:
                        pe.wait_ge(silu_done, k - 1)
                    three(bank[k % 2][:, :], WGh[:, c, :], WGl[:, c, :], xh, xl).then_inc(g_full, 1)
                    if k >= 2:
                        pe.wait_ge(t2_done, k - 1)
                    three(bank[2 + k % 2][:, :], WUh[:, c, :], WUl[:, c, :], xh, xl).then_inc(u_full, 1)
                if kind == "down":
                    k = s[1]
                    n, c = k // CH, k % CH
                    pe.wait_ge(alo_done, k + 1)
                    if k < CH and c % WCH == 0:
                        pe.wait_ge(wl_pool, c // WCH + 1)
                    if n and c == 0:
                        pe.wait_ge(y_free, n)
                    three(OACC[:, :], WDh[:, c, :], WDl[:, c, :], ah[k % 2][:, :], alo[k % 2][:, :],
                          start=(c == 0), stop=(c == CH - 1)).then_inc(down_done, 1)
                if kind == "yT":
                    n = s[1]
                    t = turn_of[s]
                    pe.wait_ge(y_free, n + 1)
                    m = turn(t)
                    for i in range(NT):
                        r = pe.transpose(m[:, i * P:i * P + P], YT[:, i * P:i * P + P], ident[:, :])
                    r.then_inc(m_full[t % 3], 1)
                if kind == "bqk":
                    _, b, j = s
                    t = turn_of[s]
                    wait_free(pe, turn_of["xT", "B", b])
                    wh, wl = swide(C_BQKV + P * j, P)
                    three(turn(t)[:, :], wh, wl, xhS[:, :], xlS[:, :]).then_inc(m_full[t % 3], 1)
                if kind == "bv":
                    b = s[1]
                    t = turn_of[s]
                    wh, wl = swide(C_BQKV + 2 * P, P)
                    m = turn(t)
                    for i in range(NT):
                        a = slice(i * P, i * P + P)
                        r = three(m[:, a], xhS[:, a], xlS[:, a], wh, wl)
                    r.then_inc(m_full[t % 3], 1)
                if kind == "bs":
                    _, b, i = s
                    t = turn_of[s]
                    pe.wait_ge(qkl_ready, 2 * b + 2)
                    a = slice(i * P, i * P + P)
                    three(turn(t)[:, :], qh[:, a], ql[:, a], kh[:, :], kl[:, :]).then_inc(m_full[t % 3], 1)
                if kind == "bpT":
                    _, b, j = s
                    t = turn_of[s]
                    pe.wait_ge(bexp_done, NT * (b + 1))
                    m = turn(t)
                    for i in range(NT):
                        r = pe.transpose(m[:, i * P:i * P + P], Sb[:, i, j * P:j * P + P], ident[:, :])
                    r.then_inc(m_full[t % 3], 1)
                if kind == "bo":
                    _, b, half = s
                    t = turn_of["bo", b, 0]
                    if half == 0:
                        pe.wait_ge(v_ready, b + 1)
                    m = turn(t)
                    for j in (2 * half, 2 * half + 1):
                        wait_free(pe, turn_of["bpT", b, j])
                        r = three(m[:, :], vh[:, j, :], vl[:, j, :], PTh[:, j, :], PTl[:, j, :],
                                  start=(j == 0), stop=(j == NT - 1))
                    if half == 1:
                        r.then_inc(m_full[t % 3], 1)
                if kind == "by":
                    b = s[1]
                    t = turn_of[s]
                    wait_free(pe, turn_of["bo", b, 0])
                    m = turn(t)
                    wh, wl = swide(C_BPROJ, P)
                    for i in range(NT):
                        a = slice(i * P, i * P + P)
                        r = three(m[:, a], oTh[:, a], oTl[:, a], wh, wl)
                    r.then_inc(m_full[t % 3], 1)


def kernel(L0_attn_a_x, L0_attn_a_norm_weight, L0_attn_a_w_qkv, L0_attn_a_temperature, L0_attn_a_w_out,
           L0_attn_b_W_qkv, L0_attn_b_b_qkv, L0_attn_b_W_proj, L0_attn_b_b_proj, L0_ffn_router_w,
           L0_ffn_actor_w1, L0_ffn_actor_b1, L0_ffn_actor_w2, L0_ffn_actor_b2, L0_ffn_gate_w, L0_ffn_up_w,
           L0_ffn_down_w):
    import numpy as np
    import concourse.bacc as bacc
    from concourse.bass_utils import run_bass_kernel_spmd

    a = lambda v: np.asarray(v)
    small = np.zeros((P, C_ALL), np.float32)
    small[:, C_QKV:C_QKV + 384] = a(L0_attn_a_w_qkv).T
    small[:, C_OUT:C_OUT + P] = a(L0_attn_a_w_out).T
    small[:, C_BQKV:C_BQKV + 384] = a(L0_attn_b_W_qkv)
    small[:, C_BPROJ:C_BPROJ + P] = a(L0_attn_b_W_proj)
    small[:, C_ROUTER:C_ROUTER + E] = a(L0_ffn_router_w).T
    small[:, C_ACTOR:C_ACTOR + AH] = a(L0_ffn_actor_w1).T
    columns = np.zeros((P, 6), np.float32)
    columns[:, 0] = a(L0_attn_a_norm_weight)
    columns[:, 1:4] = a(L0_attn_b_b_qkv).reshape(3, P).T
    columns[:AH, 4] = a(L0_ffn_actor_b1)
    columns[:, 5] = np.repeat(a(L0_attn_a_temperature).reshape(H), DH)
    row = np.zeros((272,), np.float32)
    row[0:P] = a(L0_attn_b_b_qkv)[2 * P:]
    row[P:2 * P] = a(L0_attn_b_b_proj)
    row[256:262] = a(L0_ffn_actor_b2)

    def hidden_cols(w):
        return np.ascontiguousarray(a(w).reshape(E, CH, 16, D).transpose(3, 1, 0, 2).reshape(D, CH * P))

    arrays = {
        "x": np.ascontiguousarray(a(L0_attn_a_x)),
        "small": small,
        "gate": hidden_cols(L0_ffn_gate_w),
        "up": hidden_cols(L0_ffn_up_w),
        "down": np.ascontiguousarray(a(L0_ffn_down_w).reshape(E, D, CH, 16).transpose(0, 3, 2, 1).reshape(P, CH * D)),
        "w2": np.ascontiguousarray(a(L0_ffn_actor_w2).T),
        "columns": columns,
        "row": row,
    }
    nc = bacc.Bacc("TRN2", target_bir_lowering=False, num_devices=1)
    args = [nc.dram_tensor(f"in_{n}", v.shape, F32, kind="ExternalInput").ap() for n, v in arrays.items()]
    args.append(nc.dram_tensor("out", arrays["x"].shape, F32, kind="ExternalOutput").ap())
    build(nc, *args)
    r = run_bass_kernel_spmd(nc, [{f"in_{n}": v for n, v in arrays.items()}], core_ids=[0])
    return r.results[0]["out"]
```

```python
from contextlib import ExitStack

import concourse.bass as bass
from concourse import mybir

F32 = mybir.dt.float32
F32R = mybir.dt.float32r
BF16 = mybir.dt.bfloat16
ALU = mybir.AluOpType
ACT = mybir.ActivationFunctionType
AX_X = mybir.AxisListType.X

P = 128
NB = 4
T = 512
NT = T // P
D = 128
H, DH = 8, 16
E, I, CH = 8, 336, 21
KMAX, AH = 6, 50
LN_EPS, RMS_EPS = 1e-5, 1e-6
B_SCALE = 8 ** -0.5 / 10
X10, X25, X85, X95 = (-2.1972245773362196, -1.0986122886681098, 1.7346010553881064, 2.9444389791664403)
HL_LAG = 2
LAG = 4
NSL, NT2 = 2, 4
WCH = 3
WCOLS = WCH * P
NPIECES = 3 * CH // WCH
NEG = -1e30

C_QKV, C_OUT, C_BPROJ, C_ROUTER, C_BQKV, C_ACTOR = 0, 384, 512, 640, 648, 1032
C_ALL = C_ACTOR + P


A_STEPS = [(0, "stats"), (1, "xn"), (3, "xT"), (5, "aqk", 0), (6, "aqk", 1), (8, "av"), (10, "asim"),
           (10, "ass"), (12, "ascale"), (14, "asT"), (14, "amax"), (15, "aexp"), (17, "aT"),
           (19, "aav"), (21, "y")]
B_STEPS = [(0, "stats"), (2, "xn"), (4, "xT"), (4, "xl"), (6, "bqk", 0), (7, "bqk", 1), (7, "bqkl", 0),
           (7, "bqkl", 1), (10, "bs", 0), (10, "bsp", 0, 0), (11, "bsp", 0, 1), (13, "bsp", 0, 2),
           (15, "bs", 1), (14, "bsp", 0, 3), (15, "bsp", 1, 0), (16, "bv"), (15, "bsp", 1, 1),
           (17, "bsp", 1, 2), (18, "bs", 2), (18, "bsp", 1, 3), (19, "bsp", 2, 0), (19, "bexp", 0),
           (19, "bexp", 1), (20, "bsp", 2, 1), (21, "bsp", 2, 2), (22, "bs", 3), (25, "bsp", 2, 3),
           (22, "bsp", 3, 0), (25, "bsp", 3, 1), (26, "bsp", 3, 2), (27, "bsp", 3, 3), (28, "bexp", 2),
           (27, "bexp", 3), (30, "bpT", 0), (31, "bpT", 1), (30, "bpT", 2), (32, "bo", 0),
           (32, "bpT", 3), (33, "bo", 1), (35, "bo", 2), (32, "bo", 3), (36, "by"), (36, "byx")]
F_STEPS = [(0, "stats"), (1, "xn"), (3, "xT"), (4, "xl"), (6, "route"), (7, "rexp"), (7, "inner", 0),
           (10, "inner", 1), (9, "rsum"), (12, "rrank"), (12, "tanh"), (12, "gelu"), (14, "act"),
           (14, "actk"), (18, "sbc")]
A_STARTS = (-42, -26, 1, 21)
B_STARTS = (25, 48, 67, 90)
PIECES_FROM, PIECES_LEFT = 5, 12
GU_AFTER = {("tanh", 0): 0, ("act", 0): 1}
SHIFTS = 1
F_AHEAD = 22


TURNS = dict(xT=1, aqk=1, av=1, asim=1, asT=1, aT=1, aav=1, y=1, route=2, act=1, sbc=1, yT=1,
             bqk=1, bv=1, bs=1, bpT=1, bo=1, by=1)

FREED_BY = dict(asim="ascale", asT="amax", act="actk", by="byx")
COST = dict(stats=(0, 0, 1.2), xn=(0, 0, 1.1), xT=(.4, .5, 0), xl=(0, 0, .6), aqk=(.9, 1, 0), av=(.9, .5, 0),
            asim=(1.3, 0, 0), ass=(0, 0, .1), ascale=(0, 0, .3), asT=(.1, 0, 0), amax=(0, 0, .5), aexp=(0, 3, 0),
            aT=(.1, .2, .1), aav=(.9, .5, 0), y=(.9, 0, .6), route=(2, 1.1, .3), rexp=(0, 2.7, 0),
            rsum=(0, 0, 1.3), rrank=(0, 0, 1.1), tanh=(0, .5, 0), gelu=(0, 0, .6), act=(.9, 0, 0), actk=(0, 0, 1.3),
            sbc=(.4, .5, 0), yT=(.4, 0, .6), bqk=(.7, 1, 0), bs=(.7, .5, 0), bsp=(0, 0, .9),
            bv=(.7, 0, .6), bexp=(0, 1.2, 0), bpT=(.4, .5, 0), bo=(.9, .1, 0),
            by=(.9, 0, 0), byx=(0, 0, 1.4))
DEBT = 0.1


def thread(kind, b, steps, start):
    norm = ("stats", "xn", "xT", "xl")
    return [start, [(s[0], (s[1], kind, b) if s[1] in norm else (s[1], b) + s[2:])
                    for s in steps], 0]


def needs(s):
    kind, b = s[0], s[-1] if s[0] in ("stats", "xn", "xT", "xl") else s[1]
    prev = b - 1
    if kind == "stats":
        return {"A": [], "F": [("y", b) if b < NB else ("byx", b - NB)], "B": [("yT", b)]}[s[1]]
    if kind == "xT" and s[1] == "A":
        return [("av", prev)]
    if kind in ("xT", "xl") and s[1] == "B":
        return [("bv", prev)]
    if kind == "yT":
        return [("down", CH * (b + 1) - 1)]
    if kind == "bexp":
        return [("byx", prev), ("bsp", b, s[-1], 3)]
    if kind == "bpT":
        return [("bo", prev, NT - 1)] + [("bexp", b, i) for i in range(NT)]
    return {"aqk": [("asim", prev)], "av": [("aav", prev)], "ass": [("ascale", prev)],
            "ascale": [("asT", prev), ("amax", prev)], "amax": [("aexp", prev)], "aexp": [("aT", prev)],
            "aT": [("aav", prev)], "aav": [("y", prev)],
            "bqk": [("bs", prev, NT - 1)], "bs": [("bpT", prev, NT - 1)], "bv": [("bo", prev, NT - 1)],
            "bo": [("by", prev)],
            "route": [("act", prev)], "rsum": [("actk", prev)], "actk": [("sbc", prev)]}.get(kind, [])


def plan():
    last = CH * 2 * NB
    threads = [thread("F", n, F_STEPS, CH * n - F_AHEAD) for n in range(2 * NB)]
    threads += [[CH * (n + 1) + 3, [(0, ("yT", n))], 0] for n in range(2 * NB - 1)]
    threads += [thread("B", b, B_STEPS, B_STARTS[b]) for b in range(NB)]
    threads += [thread("A", b, A_STEPS, A_STARTS[b]) for b in range(NB)]
    pieces = [("wp", j) for j in range(NPIECES)]
    steps, done, order = [], set(), {}
    free_after = []
    debt = [0.0, 0.0]

    def ready(s):
        if not all(v in done or v[1] == -1 for v in needs(s)):
            return False
        if s[0] == "xn" and order[s[1:]] >= 2:
            two_before = [v for v, i in order.items() if i == order[s[1:]] - 2][0]
            if ("xT",) + two_before not in done:
                return False
        if s[0] == "stats" and len(order) >= 2:
            two_before = [v for v, i in order.items() if i == len(order) - 2][0]
            if ("xn",) + two_before not in done:
                return False
        n = 0 if s[0] == "bo" and s[2] else TURNS.get(s[0], 0)
        return all(len(free_after) + i < 3 or free_after[len(free_after) + i - 3] in done for i in range(n))

    def add(s):
        steps.append(s)
        done.add(s)
        if s[0] == "stats":
            order[s[1:]] = len(order)
        if s[0] in TURNS and not (s[0] == "bo" and s[2]):
            by = s
            if s[0] == "xT" and s[1] != "A":
                by = ("xl",) + s[1:]
            if s[0] in FREED_BY:
                by = (FREED_BY[s[0]],) + s[1:]
            if s[0] == "bo":
                by = ("bo", s[1], NT - 1)
            free_after.extend([by] * TURNS[s[0]])

    k = A_STARTS[0] - 1
    while k < last - 1:
        if k + 1 < 0 or (k + 1) % CH or ("sbc", (k + 1) // CH) in done:
            k += 1
        else:
            for th in threads:
                th[0] -= th[0] <= k
        if k >= 0 and ("um", k) not in done:
            if k >= 2:
                add(("gu", k))
            add(("um", k))
            if k >= LAG:
                add(("down", k - LAG))
            if k >= HL_LAG:
                add(("hl", k - HL_LAG))
        pe = 1.9
        act, dve = debt[0] + 1.0, debt[1] + 1.2
        for th in threads:
            while th[1] and th[0] + th[1][0][0] <= k:
                s = th[1][0][1]
                cost = COST.get(s[0], (0, 0, 0))
                room = pe + cost[0] + DEBT
                late = (k >= 0 and th[2] < SHIFTS
                        and (act + cost[1] > room + (cost[1] > 2) * 3 or dve + cost[2] > room))
                if not ready(s) or late:
                    th[0] += 1
                    th[2] += 1
                    break
                th[1].pop(0)
                add(s)
                if s in GU_AFTER:
                    add(("gu", GU_AFTER[s]))
                pe, act, dve = pe + cost[0], act + cost[1], dve + cost[2]
        if pieces and (k >= 0 or k >= A_STARTS[0] + PIECES_FROM and len(pieces) > PIECES_LEFT):
            add(pieces.pop(0))
        debt = [max(0.0, act - pe), max(0.0, dve - pe)]
    assert not any(th[1] for th in threads)
    for k in range(last, last + LAG):
        add(("down", k - LAG))
        if k - HL_LAG < last:
            add(("hl", k - HL_LAG))
    add(("yT", 2 * NB - 1))
    return steps, order


def build(nc, x_d, small_d, gate_d, up_d, down_d, w2_d, cols_d, rows_d, out_d):
    steps, norm_no = plan()
    turn_of = {}
    turns = 0
    for s in steps:
        if s[0] in TURNS and (s[0] != "bo" or s[2] == 0):
            turn_of[s] = turns
            turns += TURNS[s[0]]
    xT_turn = {norm_no[s[1:]]: turn_of[s] for s in steps if s[0] == "xT"}
    split_no = {s[1:]: i for i, s in enumerate(s for s in steps if s[0] == "xT" and s[1] != "A")}
    wrote = {("A", b): None for b in range(NB)}
    wrote |= {("F", b): ("y", b) for b in range(NB)} | {("B", b): ("yT", b) for b in range(NB)}
    wrote |= {("F", NB + b): ("by", b) for b in range(NB)}

    with ExitStack() as ctx:
        base = (nc.sbuf_base + 63) // 64 * 64
        cursor = [base]

        def sb(name, shape, dt=F32):
            size = 1
            for n in shape[1:]:
                size *= n
            size = (size * (2 if dt == BF16 else 4) + 31) // 32 * 32
            t = nc.alloc_sbuf_tensor_at(name, shape, dt, offset=cursor[0])
            cursor[0] += size
            return t

        X = sb("X", [P, NB * NT, D])
        WGh, WGl = (sb(n, [P, CH, P], F32R) for n in ("WGh", "WGl"))
        WUh, WUl = (sb(n, [P, CH, P], F32R) for n in ("WUh", "WUl"))
        WDh, WDl = (sb(n, [P, CH, P], F32R) for n in ("WDh", "WDl"))
        raw = sb("raw", [P, C_ALL])
        SWh, SWl = (sb(n, [P, C_ALL - C_BQKV], F32R) for n in ("SWh", "SWl"))
        ident = sb("ident", [P, P])
        w2 = sb("w2", [AH, KMAX + 2])
        cols = sb("cols", [P, 6])
        rows = sb("rows", [P, 272])
        bq = sb("bq", [P, 1])
        etemp = sb("etemp", [P, 1])
        ones = sb("ones", [P, 1])
        hmask = sb("hmask", [P, P])
        nhalf = sb("nhalf", [P, NT])
        xhS, xlS = (sb(n, [P, T], F32R) for n in ("xhS", "xlS"))
        xhF = [sb(f"xhF{i}", [P, T], F32R) for i in range(2)]
        xlF = [sb(f"xlF{i}", [P, T], F32R) for i in range(2)]
        xns = [sb(f"xn{i}", [P, NT, D]) for i in range(2)]
        bst = sb("bst", [P, NT, 6])
        mvs = [sb(f"mv{i}", [P, NT, 2]) for i in range(2)]
        rstds = [sb(f"rstd{i}", [P, NT]) for i in range(2)]
        rts = [sb(f"rt{i}", [P, NT]) for i in range(2)]
        router = sb("router", [P, 2 * E], F32R)
        logits = sb("logits", [P, NT, E])
        pe_ = sb("pe_", [P, NT, E])
        pr = sb("pr", [P, NT, E])
        p4 = sb("p4", [P, 5, NT])
        gt = sb("gt", [P, NT, E, E], BF16)
        ge = sb("ge", [P, NT, E, E], BF16)
        tri = sb("tri", [P, E, E], BF16)
        rk = sb("rk", [P, NT, E])
        al_ = sb("al_", [P, NT, KMAX])
        av_ = sb("av_", [P, NT, KMAX])
        kidx = sb("kidx", [P, NT, KMAX])
        sx = sb("sx", [P, NT, E, P // E])
        xa, hq = (sb(n, [AH, T]) for n in ("xa", "hq"))
        YT = sb("YT", [P, T])
        sbc = [sb(f"sbc{i}", [P, T]) for i in range(2)]
        sl = [sb(f"sl{i}", [P, T]) for i in range(NSL)]
        t2 = [sb(f"t2{i}", [P, T]) for i in range(NT2)]
        ah = [sb(f"ah{i}", [P, T], F32R) for i in range(2)]
        alo = [sb(f"alo{i}", [P, T], F32R) for i in range(2)]
        xaT = sb("xaT", [P, T])
        qk = sb("qk", [P, NT, 2, P])
        sq = sb("sq", [P, NT, 2, P])
        vT = sb("vT", [P, T])
        oA = sb("oA", [P, T])
        ss, rs = (sb(n, [P, 2]) for n in ("ss", "rs"))
        simT, sim, attn, attnT = (sb(n, [P, P]) for n in ("simT", "sim", "attn", "attnT"))
        qn, amx, ars, ari = (sb(n, [P, 1]) for n in ("qn", "amx", "ars", "ari"))
        mark = cursor[0]
        stage = [sb(f"stage{i}", [P, WCOLS]) for i in range(NPIECES)]
        end = cursor[0]
        cursor[0] = mark
        qF, kF = (sb(n, [P, T]) for n in ("qF", "kF"))
        qh, ql, kh, kl = (sb(n, [P, T], F32R) for n in ("qh", "ql", "kh", "kl"))
        v = sb("v", [P, NT, D])
        Sb = sb("Sb", [P, NT, T])
        mk = [sb(f"mk{i}", [P, T], BF16) for i in range(4)]
        PT = sb("PT", [P, NT, T])
        oT = sb("oT", [P, T])
        bmx = sb("bmx", [P, NT])
        brs = sb("brs", [P, NT])
        bri = sb("bri", [P, NT])
        bt = sb("bt", [P, NT, D])
        cursor[0] = max(end, cursor[0])
        assert cursor[0] <= nc.sbuf_usable_end, cursor[0] - nc.sbuf_usable_end

        bank = [ctx.enter_context(nc.psum_tensor(f"bank{i}", [P, 512], F32)) for i in range(8)]
        OACC = bank[7]

        def sem(name):
            return ctx.enter_context(nc.semaphore(name))

        x_loaded = [sem(f"x_loaded{b}") for b in range(NB)]
        small_loaded = sem("small_loaded")
        rows_loaded = sem("rows_loaded")
        stage_loaded = [sem(f"stage_loaded{i}") for i in range(NPIECES)]
        consts_ready = sem("consts_ready")
        pool_did = sem("pool_did")
        dve_did = sem("dve_did")
        etemp_ready = sem("etemp_ready")
        bq_ready = sem("bq_ready")
        wn_ready = sem("wn_ready")
        swh_ready, swl_ready = sem("swh_ready"), sem("swl_ready")
        wh_ready, wl_dve, wl_pool = sem("wh_ready"), sem("wl_dve"), sem("wl_pool")
        stats_ready, rstd_ready, xn_ready, xh_ready = (sem(n) for n in ("stats_ready", "rstd_ready", "xn_ready", "xh_ready"))
        m_full = [sem(f"m_full{i}") for i in range(3)]
        m_free = [sem(f"m_free{i}") for i in range(3)]
        sums_ready, norms_ready, simx_ready, aexp_done, ari_ready = (
            sem(n) for n in ("sums_ready", "norms_ready", "simx_ready", "aexp_done", "ari_ready"))
        exp8_ready, factor_ready, inner_ready, th_ready, g_ready, sx_ready = (
            sem(n) for n in ("exp8_ready", "factor_ready", "inner_ready", "th_ready", "g_ready", "sx_ready"))
        pr_ready, chosen_ready = sem("pr_ready"), sem("chosen_ready")
        pe_sub = sem("pe_sub")
        g_full, silu_done, u_full, t2_done, a_done = (sem(n) for n in ("g_full", "silu_done", "u_full", "t2_done", "a_done"))
        ahi_done, alo_done, down_done, y_free = (sem(n) for n in ("ahi_done", "alo_done", "down_done", "y_free"))
        qf_ready, qkl_ready = sem("qf_ready"), sem("qkl_ready")
        sp_ready, bexp_done = sem("sp_ready"), sem("bexp_done")
        mk_ready = sem("mk_ready")
        stored = sem("stored")

        def m_bank(t):
            return bank[4 + t % 3]

        def wait_full(eng, t):
            eng.wait_ge(m_full[t % 3], t // 3 + 1)

        def wait_free(eng, t):
            eng.wait_ge(m_free[t % 3], t // 3 + 1)

        def n_free(t):
            return m_free[t % 3]

        def piece_of(j):
            hi, lo = ((WGh, WGl), (WUh, WUl), (WDh, WDl))[j % 3]
            at = slice(j // 3 * WCOLS, j // 3 * WCOLS + WCOLS)
            return (w[:, :, :].rearrange("p c n -> p (c n)")[:, at] for w in (hi, lo))

        block = ctx.enter_context(nc.Block())

        @block.sync
        def _(sp):
            xv = x_d.rearrange("b (i p) c -> p b i c", p=P)
            sp.dma_start(X[:, 0:NT, :], xv[:, 0]).then_inc(x_loaded[0], 16)
            sp.dma_start(raw[:, :], small_d).then_inc(small_loaded, 16)
            sp.dma_start(cols[:, :], cols_d).then_inc(small_loaded, 16)
            sp.dma_start(X[:, NT:2 * NT, :], xv[:, 1]).then_inc(x_loaded[1], 16)
            sp.dma_start(rows[:, :], rows_d.partition_broadcast(P)).then_inc(rows_loaded, 16)
            sp.dma_start(w2[:, 0:KMAX], w2_d).then_inc(small_loaded, 16)
            for s in steps:
                if s[0] == "wp":
                    j = s[1]
                    at = j // 3 * WCOLS
                    sp.dma_start(stage[j ][:, :], (gate_d, up_d, down_d)[j % 3][:, at:at + WCOLS])\
                      .then_inc(stage_loaded[j ], 16)
                    if j in (8, 9):
                        b = j - 6
                        sp.dma_start(X[:, NT * b:NT * b + NT, :], xv[:, b]).then_inc(x_loaded[b], 16)
            for b in range(NB):
                wait_free(sp, turn_of["yT", NB + b])
                sp.dma_start(out_d.rearrange("b (i p) c -> p b i c", p=P)[:, b], X[:, NT * b:NT * b + NT, :])\
                  .then_inc(stored, 16)
            sp.wait_ge(stored, 16 * NB)

        @block.gpsimd
        def _(pool):
            did = [0]

            def chain(ins):
                did[0] += 1
                ins.then_inc(pool_did, 1)
                pool.wait_ge(pool_did, did[0])

            def head_mask():
                for e in range(H):
                    own = hmask[:, e * DH:e * DH + DH]
                    chain(pool.memset(own, 0.0))
                    chain(pool.affine_select(out=own, in_=own, compare_op=ALU.is_ge, fill=NEG, base=-e * DH,
                                             pattern=[[0, DH]], channel_multiplier=1))
                    r = pool.affine_select(out=own, in_=own, compare_op=ALU.is_ge, fill=NEG, base=e * DH + DH - 1,
                                           pattern=[[0, DH]], channel_multiplier=-1)
                r.then_inc(consts_ready, 1)

            chain(pool.memset(ident[:, :], 0.0))
            chain(pool.affine_select(out=ident[:, :], in_=ident[:, :], compare_op=ALU.not_equal, fill=1.0,
                                     base=0, pattern=[[-1, P]], channel_multiplier=1))
            pool.memset(ones[:, :], 1.0)
            pool.memset(nhalf[:, :], -0.5).then_inc(consts_ready, 1)

            for s in steps:
                kind = s[0]
                if kind == "stats":
                    _, what, b = s
                    seq = norm_no[what, b]
                    if seq == 0:
                        pool.wait_ge(consts_ready, 1)
                    pool.wait_ge(stats_ready, seq + 1)
                    mv, rt, rstd = mvs[seq % 2], rts[seq % 2], rstds[seq % 2]
                    if seq >= 2:
                        pool.wait_ge(xn_ready, seq - 1)
                    by, more = (1.0 + RMS_EPS, RMS_EPS * LN_EPS) if what == "A" else (1.0, LN_EPS)
                    chain(pool.tensor_scalar(rt[:, :], mv[:, :, 1], by, more, ALU.mult, ALU.add))
                    pool.tensor_tensor(rstd[:, :], rt[:, :], nhalf[:, :], ALU.pow).then_inc(rstd_ready, 1)
                    if seq == 0:
                        head_mask()
                if kind == "ass":
                    b = s[1]
                    pool.wait_ge(sums_ready, b + 1)
                    if b:
                        wait_free(pool, turn_of["asT", b - 1])
                    pool.tensor_tensor(rs[:, :], ss[:, :], nhalf[:, 0:2], ALU.pow).then_inc(norms_ready, 1)
                if kind == "bqkl":
                    _, b, j = s
                    wait_free(pool, turn_of["bqk", b, j])
                    full, hi, lo = ((qF, qh, ql), (kF, kh, kl))[j]
                    pool.tensor_tensor(lo[:, :], full[:, :], hi[:, :].bitcast(F32), ALU.subtract).then_inc(qkl_ready, 1)
                if kind == "actk":
                    n = s[1]
                    pool.wait_ge(chosen_ready, n + 1)
                    if n:
                        wait_full(pool, turn_of["sbc", n - 1])
                    pool.tensor_tensor(sx[:, :, :, :], rk[:, :, :].unsqueeze(3).to_broadcast([P, NT, E, P // E]),
                                       pr[:, :, :].unsqueeze(3).to_broadcast([P, NT, E, P // E]), ALU.mult).then_inc(sx_ready, 1)
                if kind == "wp" and s[1] % 3 == 2:
                    j = s[1]
                    pool.wait_ge(wh_ready, j + 1)
                    hi, lo = piece_of(j)
                    pool.tensor_tensor(lo, stage[j ][:, :], hi.bitcast(F32), ALU.subtract).then_inc(wl_pool, 1)
                if kind == "inner" and s[2] == 0:
                    wait_free(pool, turn_of["route", s[1]] + 1)
                    pool.tensor_scalar(hq[:, :], hq[:, :], 0.044715, 1.0, ALU.mult, ALU.add).then_inc(factor_ready, 1)
                if kind == "inner" and s[2] == 1:
                    pool.wait_ge(factor_ready, s[1] + 1)
                    pool.tensor_tensor(hq[:, :], hq[:, :], xa[:, :], ALU.mult).then_inc(inner_ready, 1)
                if kind == "um":
                    k = s[1]
                    pool.wait_ge(t2_done, k + 1)
                    pool.wait_ge(silu_done, k + 1)
                    pool.tensor_tensor(t2[k % NT2][:, :], t2[k % NT2][:, :], sl[k % NSL][:, :], ALU.mult).then_inc(a_done, 1)

        @block.scalar
        def _(act):
            act.wait_ge(small_loaded, 48)
            act.activation(etemp[:, :], cols[:, 5:6], ACT.Exp).then_inc(etemp_ready, 1)
            act.activation(SWh[:, :], raw[:, C_BQKV:C_ALL], ACT.Copy).then_inc(swh_ready, 1)
            act.activation(router[:, 0:E], raw[:, C_ROUTER:C_ROUTER + E], ACT.Copy).then_inc(swh_ready, 1)
            act.activation(bq[:, :], cols[:, 1:2], ACT.Copy, scale=B_SCALE).then_inc(bq_ready, 1)

            for s in steps:
                kind = s[0]
                if kind == "xT":
                    _, what, b = s
                    t = turn_of[s]
                    wait_full(act, t)
                    if what == "A":
                        if b:
                            wait_full(act, turn_of["av", b - 1])
                        act.activation(xaT[:, :], m_bank(t)[:, :], ACT.Copy).then_inc(n_free(t), 1)
                        continue
                    if what == "F" and b >= 2:
                        act.wait_ge(u_full, CH * (b - 1))
                    if what == "B" and b:
                        wait_full(act, turn_of["bv", b - 1])
                    dst = xhF[b % 2] if what == "F" else xhS
                    act.activation(dst[:, :], m_bank(t)[:, :], ACT.Copy).then_inc(xh_ready, 1)
                if kind == "aqk":
                    _, b, j = s
                    t = turn_of[s]
                    if b:
                        wait_full(act, turn_of["asim", b - 1])
                    wait_full(act, t)
                    tiles = m_bank(t)[:, :].rearrange("p (i r c) -> p i r c", i=2, r=2)
                    act.activation(sq[:, 2 * j:2 * j + 2, :, :], tiles, ACT.Square)
                    act.activation(qk[:, 2 * j:2 * j + 2, :, :], tiles, ACT.Copy).then_inc(n_free(t), 1)
                if kind == "av":
                    b = s[1]
                    t = turn_of[s]
                    wait_full(act, t)
                    if b:
                        wait_full(act, turn_of["aav", b - 1])
                    act.activation(vT[:, :], m_bank(t)[:, :], ACT.Copy).then_inc(n_free(t), 1)
                if kind == "aexp":
                    b = s[1]
                    act.wait_ge(simx_ready, b + 1)
                    if b:
                        wait_full(act, turn_of["aT", b - 1])
                    act.activation(attn[:, :], sim[:, :], ACT.Exp, bias=amx[:, 0:1], accum_out=ars[:, 0:1])\
                       .then_inc(aexp_done, 1)
                if kind == "aT":
                    b = s[1]
                    t = turn_of[s]
                    wait_full(act, t)
                    act.activation(attnT[:, :], m_bank(t)[:, 0:P], ACT.Copy).then_inc(n_free(t), 1)
                if kind == "aav":
                    b = s[1]
                    t = turn_of[s]
                    wait_full(act, t)
                    if b:
                        wait_full(act, turn_of["y", b - 1])
                    act.wait_ge(ari_ready, b + 1)
                    act.activation(oA[:, :], m_bank(t)[:, :], ACT.Copy, scale=ari[:, 0:1]).then_inc(n_free(t), 1)
                if kind == "wp":
                    j = s[1]
                    act.wait_ge(stage_loaded[j ], 16)
                    hi, _lo = piece_of(j)
                    act.activation(hi, stage[j ][:, :], ACT.Copy).then_inc(wh_ready, 1)
                if kind == "rexp":
                    act.wait_ge(pe_sub, s[1] + 1)
                    act.activation(pe_[:, :, :], pe_[:, :, :], ACT.Exp).then_inc(exp8_ready, 1)
                if kind == "route":
                    n = s[1]
                    t = turn_of[s]
                    wait_full(act, t + 1)
                    if n:
                        wait_full(act, turn_of["act", n - 1])
                    act.activation(xa[:, :], m_bank(t + 1)[0:AH, :], ACT.Identity, bias=cols[0:AH, 4:5])
                    act.activation(hq[:, :], m_bank(t + 1)[0:AH, :], ACT.Square, bias=cols[0:AH, 4:5])\
                       .then_inc(n_free(t + 1), 1)
                if kind == "tanh":
                    n = s[1]
                    act.wait_ge(inner_ready, n + 1)
                    act.activation(hq[:, :], hq[:, :], ACT.Tanh, scale=0.7978845608028654).then_inc(th_ready, 1)
                if kind == "sbc":
                    n = s[1]
                    t = turn_of[s]
                    wait_full(act, t)
                    if n >= 2:
                        act.wait_ge(t2_done, CH * (n - 1))
                    act.activation(sbc[n % 2][:, :], m_bank(t)[:, :], ACT.Copy).then_inc(n_free(t), 1)
                if kind == "gu":
                    k = s[1]
                    act.wait_ge(g_full, k + 1)
                    if k >= NSL:
                        act.wait_ge(a_done, k - NSL + 1)
                    act.activation(sl[k % NSL][:, :], bank[k % 2][:, :], ACT.Silu).then_inc(silu_done, 1)
                if kind == "hl":
                    k = s[1]
                    act.wait_ge(a_done, k + 1)
                    if k >= 2:
                        act.wait_ge(down_done, k - 1)
                    act.activation(ah[k % 2][:, :], t2[k % NT2][:, :], ACT.Copy).then_inc(ahi_done, 1)
                if kind == "down" and s[1] % CH == CH - 1:
                    n = s[1] // CH
                    act.wait_ge(down_done, CH * (n + 1))
                    if n:
                        wait_full(act, turn_of["yT", n - 1])
                    act.activation(YT[:, :], OACC[:, :], ACT.Copy).then_inc(y_free, 1)
                if kind == "bqk":
                    _, b, j = s
                    t = turn_of[s]
                    if b == 0 and j == 0:
                        act.wait_ge(bq_ready, 1)
                    if b:
                        wait_full(act, turn_of["bs", b - 1, NT - 1])
                        act.wait_ge(qkl_ready, 2 * b)
                    wait_full(act, t)
                    full, hi = ((qF, qh), (kF, kh))[j]
                    if j == 0:
                        act.activation(full[:, :], m_bank(t)[:, :], ACT.Identity, bias=bq[:, 0:1], scale=B_SCALE)\
                           .then_inc(qf_ready, 1)
                    else:
                        act.activation(full[:, :], m_bank(t)[:, :], ACT.Identity, bias=cols[:, 2:3]).then_inc(qf_ready, 1)
                    act.wait_ge(qf_ready, 2 * b + j + 1)
                    act.activation(hi[:, :], full[:, :], ACT.Copy).then_inc(n_free(t), 1)
                if kind == "bs":
                    _, b, i = s
                    t = turn_of[s]
                    wait_full(act, t)
                    if b:
                        wait_full(act, turn_of["bpT", b - 1, NT - 1])
                    act.activation(Sb[:, i, :], m_bank(t)[:, :], ACT.Copy).then_inc(n_free(t), 1)
                if kind == "bexp":
                    _, b, i = s
                    act.wait_ge(sp_ready, NT * b + i + 1)
                    act.activation(Sb[:, i, :], Sb[:, i, :], ACT.Exp, bias=bmx[:, i:i + 1],
                                   accum_out=brs[:, i:i + 1]).then_inc(bexp_done, 1)
                if kind == "bpT":
                    _, b, j = s
                    t = turn_of[s]
                    wait_full(act, t)
                    if b:
                        wait_full(act, turn_of["bo", b - 1, 0])
                    act.activation(PT[:, j, :], m_bank(t)[:, :], ACT.Copy).then_inc(n_free(t), 1)
                if kind == "bo" and s[2] == NT - 1:
                    b = s[1]
                    t = turn_of["bo", b, 0]
                    wait_full(act, t)
                    if b:
                        wait_full(act, turn_of["by", b - 1])
                    act.activation(oT[:, :], m_bank(t)[:, :], ACT.Copy).then_inc(n_free(t), 1)

        @block.vector
        def _(dve):
            did = [0]

            def chain(ins):
                did[0] += 1
                ins.then_inc(dve_did, 1)
                dve.wait_ge(dve_did, did[0])

            for e in range(E):
                if e:
                    dve.memset(tri[:, e, 0:e], 1.0)
                dve.memset(tri[:, e, e:E], 0.0)
            for j in range(KMAX):
                r = dve.memset(kidx[:, :, j:j + 1], float(j + 1))
            chain(r)

            for s in steps:
                kind = s[0]
                if kind == "stats":
                    _, what, b = s
                    q = b % NB
                    seq = norm_no[what, b]
                    src = wrote[what, b]
                    if src is None:
                        dve.wait_ge(x_loaded[q], 16)
                    else:
                        wait_free(dve, turn_of[src])
                    mv = mvs[seq % 2]
                    if seq:
                        dve.wait_ge(stats_ready, seq)
                    for i in range(NT):
                        r = dve.bn_stats(bst[:, i, :], X[:, NT * q + i, :])
                    chain(r)
                    for i in range(NT):
                        r = dve.bn_aggr(mv[:, i, :], bst[:, i, :])
                    r.then_inc(stats_ready, 1)
                if kind == "xn":
                    _, what, b = s
                    q = b % NB
                    seq = norm_no[what, b]
                    mv, rstd, xn = mvs[seq % 2], rstds[seq % 2], xns[seq % 2]
                    if seq >= 2:
                        wait_full(dve, xT_turn[seq - 2])
                    dve.wait_ge(rstd_ready, seq + 1)
                    for i in range(NT):
                        r = dve.tensor_scalar(xn[:, i, :], X[:, NT * q + i, :], mv[:, i, 0:1], rstd[:, i:i + 1],
                                              ALU.subtract, ALU.mult)
                    r.then_inc(xn_ready, 1)
                    if seq == 0:
                        dve.wait_ge(small_loaded, 48)
                        dve.tensor_scalar(raw[:, 0:384], raw[:, 0:384], cols[:, 0:1], None, ALU.mult).then_inc(wn_ready, 1)
                        dve.wait_ge(wn_ready, 1)
                        dve.wait_ge(swh_ready, 2)
                        dve.tensor_tensor(router[:, E:2 * E], raw[:, C_ROUTER:C_ROUTER + E],
                                          router[:, 0:E].bitcast(F32), ALU.subtract)
                        dve.tensor_tensor(SWl[:, :], raw[:, C_BQKV:C_ALL], SWh[:, :].bitcast(F32), ALU.subtract)\
                           .then_inc(swl_ready, 1)
                if kind == "xl":
                    _, what, b = s
                    t = turn_of["xT", what, b]
                    dst, hi = (xlF[b % 2], xhF[b % 2]) if what == "F" else (xlS, xhS)
                    dve.wait_ge(xh_ready, split_no[what, b] + 1)
                    if what == "B" and b:
                        wait_full(dve, turn_of["bv", b - 1])
                    dve.tensor_tensor(dst[:, :], m_bank(t)[:, :], hi[:, :].bitcast(F32), ALU.subtract).then_inc(n_free(t), 1)
                if kind == "wp" and s[1] % 3 != 2:
                    j = s[1]
                    dve.wait_ge(wh_ready, j + 1)
                    hi, lo = piece_of(j)
                    dve.tensor_tensor(lo, stage[j ][:, :], hi.bitcast(F32), ALU.subtract).then_inc(wl_dve, 1)
                if kind == "ass":
                    b = s[1]
                    t = turn_of["asim", b]
                    wait_full(dve, t)
                    if b:
                        dve.wait_ge(norms_ready, b)
                    dve.tensor_scalar(ss[:, :], m_bank(t)[:, P:P + 2], 1e-24, None, ALU.max).then_inc(sums_ready, 1)
                if kind == "ascale":
                    b = s[1]
                    t = turn_of["asim", b]
                    dve.wait_ge(norms_ready, b + 1)
                    if b == 0:
                        dve.wait_ge(etemp_ready, 1)
                    dve.tensor_tensor(qn[:, :], rs[:, 1:2], etemp[:, 0:1], ALU.mult)
                    dve.tensor_scalar(simT[:, :], m_bank(t)[:, 0:P], rs[:, 0:1], None, ALU.mult).then_inc(n_free(t), 1)
                if kind == "amax":
                    b = s[1]
                    t = turn_of["asT", b]
                    if b == 0:
                        dve.wait_ge(consts_ready, 2)
                    else:
                        dve.wait_ge(aexp_done, b)
                    wait_full(dve, t)
                    dve.scalar_tensor_tensor(sim[:, :], m_bank(t)[:, 0:P], qn[:, 0:1], hmask[:, :], ALU.mult, ALU.add)\
                       .then_inc(n_free(t), 1)
                    wait_free(dve, t)
                    dve.tensor_reduce(amx[:, 0:1], sim[:, :], AX_X, ALU.max, negate=True).then_inc(simx_ready, 1)
                if kind == "aT":
                    b = s[1]
                    dve.wait_ge(aexp_done, b + 1)
                    if b:
                        wait_free(dve, turn_of["aav", b - 1])
                    dve.reciprocal(ari[:, :], ars[:, :]).then_inc(ari_ready, 1)
                if kind in ("y", "yT"):
                    t = turn_of[s]
                    q = s[1] % NB
                    wait_full(dve, t)
                    xs = X[:, NT * q:NT * q + NT, :].rearrange("p i d -> p (i d)")
                    dve.tensor_tensor(xs, m_bank(t)[:, :], xs, ALU.add).then_inc(n_free(t), 1)
                if kind == "route":
                    n = s[1]
                    t = turn_of[s]
                    wait_full(dve, t)
                    parts = m_bank(t)[:, 0:NT * 3 * E].rearrange("p (i r e) -> p i e r", r=3, e=E)
                    dve.tensor_reduce(logits[:, :, :], parts, AX_X, ALU.add).then_inc(n_free(t), 1)
                    wait_free(dve, t)
                    chain(dve.tensor_reduce(p4[:, 0], logits[:, :, :], AX_X, ALU.max))
                    dve.tensor_tensor(pe_[:, :, :], logits[:, :, :], p4[:, 0].unsqueeze(2).to_broadcast([P, NT, E]),
                                      ALU.subtract).then_inc(pe_sub, 1)
                if kind == "rsum":
                    n = s[1]
                    if n:
                        dve.wait_ge(sx_ready, n)
                    dve.wait_ge(exp8_ready, n + 1)
                    chain(dve.tensor_reduce(p4[:, 1], pe_[:, :, :], AX_X, ALU.add))
                    chain(dve.reciprocal(p4[:, 2], p4[:, 1]))
                    chain(dve.tensor_tensor(pr[:, :, :], pe_[:, :, :], p4[:, 2].unsqueeze(2).to_broadcast([P, NT, E]), ALU.mult))
                    other = pr[:, :, :].unsqueeze(2).to_broadcast([P, NT, E, E])
                    own = pr[:, :, :].unsqueeze(3).to_broadcast([P, NT, E, E])
                    dve.tensor_tensor(gt[:, :, :, :], other, own, ALU.is_gt)
                    dve.tensor_tensor(ge[:, :, :, :], other, own, ALU.is_ge).then_inc(pr_ready, 1)
                if kind == "rrank":
                    n = s[1]
                    dve.wait_ge(pr_ready, n + 1)
                    chain(dve.tensor_tensor(ge[:, :, :, :], ge[:, :, :, :],
                                            tri[:, :, :].unsqueeze(1).to_broadcast([P, NT, E, E]), ALU.mult))
                    chain(dve.tensor_tensor(gt[:, :, :, :], gt[:, :, :, :], ge[:, :, :, :], ALU.max))
                    chain(dve.tensor_reduce(rk[:, :, :], gt[:, :, :, :], AX_X, ALU.add))
                if kind == "gelu":
                    n = s[1]
                    dve.wait_ge(th_ready, n + 1)
                    dve.scalar_tensor_tensor(hq[:, :], hq[:, :], 1.0, xa[:, :], ALU.add, ALU.mult).then_inc(g_ready, 1)
                if kind == "actk":
                    n = s[1]
                    t = turn_of["act", n]
                    if n == 0:
                        dve.wait_ge(rows_loaded, 16)
                    wait_full(dve, t)
                    lg = m_bank(t)[:, 0:NT * 8].rearrange("p (i e) -> p i e", e=8)[:, :, 0:KMAX]
                    dve.scalar_tensor_tensor(al_[:, :, :], lg, 0.5,
                                             rows[:, 256:262].unsqueeze(1).to_broadcast([P, NT, KMAX]),
                                             ALU.mult, ALU.add).then_inc(n_free(t), 1)
                    wait_free(dve, t)
                    chain(dve.tensor_scalar(al_[:, :, :], al_[:, :, :], 30.0, -30.0, ALU.min, ALU.max))
                    chain(dve.tensor_reduce(p4[:, 3], al_[:, :, :], AX_X, ALU.max))
                    chain(dve.tensor_tensor(av_[:, :, :], al_[:, :, :], p4[:, 3].unsqueeze(2).to_broadcast([P, NT, KMAX]), ALU.is_ge))
                    chain(dve.scalar_tensor_tensor(av_[:, :, :], av_[:, :, :], -16.0, kidx[:, :, :], ALU.mult, ALU.add))
                    chain(dve.tensor_reduce(p4[:, 4], av_[:, :, :], AX_X, ALU.min))
                    dve.scalar_tensor_tensor(rk[:, :, :], rk[:, :, :], -16.0,
                                             p4[:, 4].unsqueeze(2).to_broadcast([P, NT, E]), ALU.add, ALU.is_lt)\
                       .then_inc(chosen_ready, 1)
                if kind == "um":
                    k = s[1]
                    if k % CH == 0:
                        wait_free(dve, turn_of["sbc", k // CH])
                    dve.wait_ge(u_full, k + 1)
                    if k >= NT2:
                        dve.wait_ge(alo_done, k - NT2 + 1)
                    dve.tensor_tensor(t2[k % NT2][:, :], bank[2 + k % 2][:, :], sbc[k // CH % 2][:, :],
                                      ALU.mult).then_inc(t2_done, 1)
                if kind == "hl":
                    k = s[1]
                    dve.wait_ge(ahi_done, k + 1)
                    if k >= 2:
                        dve.wait_ge(down_done, k - 1)
                    dve.tensor_tensor(alo[k % 2][:, :], t2[k % NT2][:, :], ah[k % 2][:, :].bitcast(F32),
                                      ALU.subtract).then_inc(alo_done, 1)
                if kind == "bv":
                    b = s[1]
                    t = turn_of[s]
                    if b:
                        wait_full(dve, turn_of["bo", b - 1, 0])
                    wait_full(dve, t)
                    dve.tensor_tensor(v[:, :, :], m_bank(t)[:, :].rearrange("p (i d) -> p i d", d=D),
                                      rows[:, 0:P].unsqueeze(1).to_broadcast([P, NT, D]), ALU.add).then_inc(n_free(t), 1)
                if kind == "bsp":
                    _, b, i, part = s
                    x_ = Sb[:, i, :]
                    step_no = 3 * (NT * b + i)
                    if part == 0:
                        wait_free(dve, turn_of["bs", b, i])
                        dve.tensor_scalar(mk[0][:, :], x_, X10 / 10, 2.0, ALU.is_ge, ALU.mult)
                        chain(dve.tensor_scalar(mk[1][:, :], x_, X25 / 10, 7.0, ALU.is_ge, ALU.mult))
                        dve.tensor_tensor(mk[0][:, :], mk[0][:, :], mk[1][:, :], ALU.add).then_inc(mk_ready, 1)
                    if part == 1:
                        dve.tensor_scalar(mk[2][:, :], x_, X85 / 10, 5.0, ALU.is_gt, ALU.mult)
                        chain(dve.tensor_scalar(mk[3][:, :], x_, X95 / 10, 5.0, ALU.is_gt, ALU.mult))
                        dve.tensor_tensor(mk[2][:, :], mk[2][:, :], mk[3][:, :], ALU.add).then_inc(mk_ready, 1)
                    if part == 2:
                        dve.wait_ge(mk_ready, step_no + 2)
                        chain(dve.tensor_tensor(mk[0][:, :], mk[0][:, :], mk[2][:, :], ALU.add))
                        dve.scalar_tensor_tensor(x_, mk[0][:, :], 1.0, x_, ALU.add, ALU.mult).then_inc(mk_ready, 1)
                    if part == 3:
                        dve.wait_ge(mk_ready, step_no + 3)
                        dve.tensor_reduce(bmx[:, i:i + 1], x_, AX_X, ALU.max, negate=True).then_inc(sp_ready, 1)
                if kind == "bpT" and s[2] == 0:
                    dve.wait_ge(bexp_done, NT * (s[1] + 1))
                    dve.reciprocal(bri[:, :], brs[:, :])
                if kind == "byx":
                    b = s[1]
                    t = turn_of["by", b]
                    wait_full(dve, t)
                    for i in range(NT):
                        r = dve.scalar_tensor_tensor(bt[:, i, :], m_bank(t)[:, i * P:i * P + P], bri[:, i:i + 1],
                                                     rows[:, P:2 * P], ALU.mult, ALU.add)
                    chain(r)
                    xs = X[:, NT * b:NT * b + NT, :]
                    dve.tensor_tensor(xs, xs, bt[:, :, :], ALU.add).then_inc(n_free(t), 1)

        @block.tensor
        def _(pe):
            def turn(t):
                if t >= 3:
                    wait_free(pe, t - 3)
                return m_bank(t)

            def three(out, lh, ll, rh, rl, start=True, stop=True):
                pe.matmul(out, lh, rh, start=start, stop=False)
                pe.matmul(out, lh, rl, start=False, stop=False)
                return pe.matmul(out, ll, rh, start=False, stop=stop)

            def swide(c, n):
                return SWh[:, c - C_BQKV:c - C_BQKV + n], SWl[:, c - C_BQKV:c - C_BQKV + n]

            pe.wait_ge(consts_ready, 1)
            for s in steps:
                kind = s[0]
                if kind == "xT":
                    _, what, b = s
                    t = turn_of[s]
                    pe.wait_ge(xn_ready, norm_no[what, b] + 1)
                    xn = xns[norm_no[what, b] % 2]
                    m = turn(t)
                    for i in range(NT):
                        r = pe.transpose(m[:, i * P:i * P + P], xn[:, i, :], ident[:, :])
                    r.then_inc(m_full[t % 3], 1)
                if kind == "aqk":
                    _, b, j = s
                    t = turn_of[s]
                    if b == 0:
                        pe.wait_ge(wn_ready, 1)
                    wait_free(pe, turn_of["xT", "A", b])
                    m = turn(t)
                    for i in range(2):
                        r = pe.matmul(m[:, 256 * i:256 * i + 256], xaT[:, (2 * j + i) * P:(2 * j + i) * P + P],
                                      raw[:, C_QKV:C_QKV + 256], start=True, stop=True)
                    r.then_inc(m_full[t % 3], 1)
                if kind == "av":
                    b = s[1]
                    t = turn_of[s]
                    pe.matmul(turn(t)[:, :], raw[:, C_QKV + 256:C_QKV + 384], xaT[:, :], start=True, stop=True)\
                      .then_inc(m_full[t % 3], 1)
                if kind == "asim":
                    b = s[1]
                    t = turn_of[s]
                    m = turn(t)
                    wait_free(pe, turn_of["aqk", b, 0])
                    wait_free(pe, turn_of["aqk", b, 1])
                    for i in range(NT):
                        pe.matmul(m[:, 0:P], qk[:, i, 1, :], qk[:, i, 0, :], start=(i == 0), stop=(i == NT - 1))
                    for j in range(2):
                        for i in range(NT):
                            r = pe.matmul(m[:, P + j:P + j + 1], sq[:, i, 1 - j, :], ones[:, :],
                                          start=(i == 0), stop=(i == NT - 1))
                    r.then_inc(m_full[t % 3], 1)
                if kind == "asT":
                    b = s[1]
                    t = turn_of[s]
                    wait_free(pe, turn_of["asim", b])
                    pe.transpose(turn(t)[:, 0:P], simT[:, :], ident[:, :]).then_inc(m_full[t % 3], 1)
                if kind == "aT":
                    b = s[1]
                    t = turn_of[s]
                    pe.wait_ge(aexp_done, b + 1)
                    pe.transpose(turn(t)[:, 0:P], attn[:, :], ident[:, :]).then_inc(m_full[t % 3], 1)
                if kind == "aav":
                    b = s[1]
                    t = turn_of[s]
                    wait_free(pe, turn_of["aT", b])
                    pe.matmul(turn(t)[:, :], attnT[:, :], vT[:, :], start=True, stop=True).then_inc(m_full[t % 3], 1)
                if kind == "y":
                    b = s[1]
                    t = turn_of[s]
                    wait_free(pe, turn_of["aav", b])
                    m = turn(t)
                    for i in range(NT):
                        a = slice(i * P, i * P + P)
                        r = pe.matmul(m[:, a], oA[:, a], raw[:, C_OUT:C_OUT + P], start=True, stop=True)
                    r.then_inc(m_full[t % 3], 1)
                if kind == "route":
                    n = s[1]
                    t = turn_of[s]
                    if n == 0:
                        pe.wait_ge(swl_ready, 1)
                    wait_free(pe, turn_of["xT", "F", n])
                    xh, xl = xhF[n % 2], xlF[n % 2]
                    m = turn(t)
                    for i in range(NT):
                        a, o = slice(i * P, i * P + P), 3 * E * i
                        pe.matmul(m[:, o:o + 2 * E], xh[:, a], router[:, :], start=True, stop=True)
                        r = pe.matmul(m[:, o + 2 * E:o + 3 * E], xl[:, a], router[:, 0:E], start=True, stop=True)
                    r.then_inc(m_full[t % 3], 1)
                    m = turn(t + 1)
                    wh, wl = swide(C_ACTOR, P)
                    three(m[:, :], wh, wl, xh[:, :], xl[:, :]).then_inc(m_full[(t + 1) % 3], 1)
                if kind == "act":
                    n = s[1]
                    t = turn_of[s]
                    pe.wait_ge(g_ready, n + 1)
                    m = turn(t)
                    for i in range(NT):
                        r = pe.matmul(m[:, 8 * i:8 * i + KMAX], hq[:, i * P:i * P + P], w2[:, 0:KMAX], start=True, stop=True)
                    r.then_inc(m_full[t % 3], 1)
                if kind == "sbc":
                    n = s[1]
                    t = turn_of[s]
                    pe.wait_ge(sx_ready, n + 1)
                    m = turn(t)
                    for i in range(NT):
                        r = pe.transpose(m[:, i * P:i * P + P], sx[:, i, :, :].rearrange("p e r -> p (e r)"), ident[:, :])
                    r.then_inc(m_full[t % 3], 1)
                if kind == "gu":
                    k = s[1]
                    n, c = k // CH, k % CH
                    if k < CH and c % WCH == 0:
                        pe.wait_ge(wl_dve, 2 * (c // WCH) + 2)
                    if c == 0:
                        wait_free(pe, turn_of["xT", "F", n])
                    xh, xl = xhF[n % 2][:, :], xlF[n % 2][:, :]
                    if k >= 2:
                        pe.wait_ge(silu_done, k - 1)
                    three(bank[k % 2][:, :], WGh[:, c, :], WGl[:, c, :], xh, xl).then_inc(g_full, 1)
                    if k >= 2:
                        pe.wait_ge(t2_done, k - 1)
                    three(bank[2 + k % 2][:, :], WUh[:, c, :], WUl[:, c, :], xh, xl).then_inc(u_full, 1)
                if kind == "down":
                    k = s[1]
                    n, c = k // CH, k % CH
                    pe.wait_ge(alo_done, k + 1)
                    if k < CH and c % WCH == 0:
                        pe.wait_ge(wl_pool, c // WCH + 1)
                    if n and c == 0:
                        pe.wait_ge(y_free, n)
                    three(OACC[:, :], WDh[:, c, :], WDl[:, c, :], ah[k % 2][:, :], alo[k % 2][:, :],
                          start=(c == 0), stop=(c == CH - 1)).then_inc(down_done, 1)
                if kind == "yT":
                    n = s[1]
                    t = turn_of[s]
                    pe.wait_ge(y_free, n + 1)
                    m = turn(t)
                    for i in range(NT):
                        r = pe.transpose(m[:, i * P:i * P + P], YT[:, i * P:i * P + P], ident[:, :])
                    r.then_inc(m_full[t % 3], 1)
                if kind == "bqk":
                    _, b, j = s
                    t = turn_of[s]
                    wait_free(pe, turn_of["xT", "B", b])
                    wh, wl = swide(C_BQKV + P * j, P)
                    three(turn(t)[:, :], wh, wl, xhS[:, :], xlS[:, :]).then_inc(m_full[t % 3], 1)
                if kind == "bv":
                    b = s[1]
                    t = turn_of[s]
                    wh, wl = swide(C_BQKV + 2 * P, P)
                    m = turn(t)
                    for i in range(NT):
                        a = slice(i * P, i * P + P)
                        r = three(m[:, a], xhS[:, a], xlS[:, a], wh, wl)
                    r.then_inc(m_full[t % 3], 1)
                if kind == "bs":
                    _, b, i = s
                    t = turn_of[s]
                    pe.wait_ge(qkl_ready, 2 * b + 2)
                    a = slice(i * P, i * P + P)
                    three(turn(t)[:, :], qh[:, a], ql[:, a], kh[:, :], kl[:, :]).then_inc(m_full[t % 3], 1)
                if kind == "bpT":
                    _, b, j = s
                    t = turn_of[s]
                    pe.wait_ge(bexp_done, NT * (b + 1))
                    m = turn(t)
                    for i in range(NT):
                        r = pe.transpose(m[:, i * P:i * P + P], Sb[:, i, j * P:j * P + P], ident[:, :])
                    r.then_inc(m_full[t % 3], 1)
                if kind == "bo":
                    _, b, j = s
                    t = turn_of["bo", b, 0]
                    if j == 0:
                        wait_free(pe, turn_of["bv", b])
                    m = turn(t)
                    wait_free(pe, turn_of["bpT", b, j])
                    r = pe.matmul(m[:, :], v[:, j, :], PT[:, j, :], start=(j == 0), stop=(j == NT - 1))
                    if j == NT - 1:
                        r.then_inc(m_full[t % 3], 1)
                if kind == "by":
                    b = s[1]
                    t = turn_of[s]
                    wait_free(pe, turn_of["bo", b, 0])
                    m = turn(t)
                    for i in range(NT):
                        a = slice(i * P, i * P + P)
                        r = pe.matmul(m[:, a], oT[:, a], raw[:, C_BPROJ:C_BPROJ + P], start=True, stop=True)
                    r.then_inc(m_full[t % 3], 1)


def kernel(L0_attn_a_x, L0_attn_a_norm_weight, L0_attn_a_w_qkv, L0_attn_a_temperature, L0_attn_a_w_out,
           L0_attn_b_W_qkv, L0_attn_b_b_qkv, L0_attn_b_W_proj, L0_attn_b_b_proj, L0_ffn_router_w,
           L0_ffn_actor_w1, L0_ffn_actor_b1, L0_ffn_actor_w2, L0_ffn_actor_b2, L0_ffn_gate_w, L0_ffn_up_w,
           L0_ffn_down_w):
    import numpy as np
    import concourse.bacc as bacc
    from concourse.bass_utils import run_bass_kernel_spmd

    a = lambda v: np.asarray(v)
    small = np.zeros((P, C_ALL), np.float32)
    small[:, C_QKV:C_QKV + 384] = a(L0_attn_a_w_qkv).T
    small[:, C_OUT:C_OUT + P] = a(L0_attn_a_w_out).T
    small[:, C_BQKV:C_BQKV + 384] = a(L0_attn_b_W_qkv)
    small[:, C_BPROJ:C_BPROJ + P] = a(L0_attn_b_W_proj)
    small[:, C_ROUTER:C_ROUTER + E] = a(L0_ffn_router_w).T
    small[:, C_ACTOR:C_ACTOR + AH] = a(L0_ffn_actor_w1).T
    columns = np.zeros((P, 6), np.float32)
    columns[:, 0] = a(L0_attn_a_norm_weight)
    columns[:, 1:4] = a(L0_attn_b_b_qkv).reshape(3, P).T
    columns[:AH, 4] = a(L0_ffn_actor_b1)
    columns[:, 5] = np.repeat(a(L0_attn_a_temperature).reshape(H), DH)
    row = np.zeros((272,), np.float32)
    row[0:P] = a(L0_attn_b_b_qkv)[2 * P:]
    row[P:2 * P] = a(L0_attn_b_b_proj)
    row[256:262] = a(L0_ffn_actor_b2)

    def hidden_cols(w):
        return np.ascontiguousarray(a(w).reshape(E, CH, 16, D).transpose(3, 1, 0, 2).reshape(D, CH * P))

    arrays = {
        "x": np.ascontiguousarray(a(L0_attn_a_x)),
        "small": small,
        "gate": hidden_cols(L0_ffn_gate_w),
        "up": hidden_cols(L0_ffn_up_w),
        "down": np.ascontiguousarray(a(L0_ffn_down_w).reshape(E, D, CH, 16).transpose(0, 3, 2, 1).reshape(P, CH * D)),
        "w2": np.ascontiguousarray(a(L0_ffn_actor_w2).T),
        "columns": columns,
        "row": row,
    }
    nc = bacc.Bacc("TRN2", target_bir_lowering=False, num_devices=1)
    args = [nc.dram_tensor(f"in_{n}", v.shape, F32, kind="ExternalInput").ap() for n, v in arrays.items()]
    args.append(nc.dram_tensor("out", arrays["x"].shape, F32, kind="ExternalOutput").ap())
    build(nc, *args)
    r = run_bass_kernel_spmd(nc, [{f"in_{n}": v for n, v in arrays.items()}], core_ids=[0])
    return r.results[0]["out"]
```
